# Optimizing a Trainium2 kernel written in Bass

```python
import numpy as np
import jax
import jax.numpy as jnp

def _softmax(x, axis=-1):
    return jax.nn.softmax(x, axis=axis)

def _gelu(x):
    return jax.nn.gelu(x, approximate=True)

def _silu(x):
    return jax.nn.silu(x)

def _sigmoid(x):
    return jax.nn.sigmoid(x)

def _layernorm(x, axis=-1, eps=1e-05):
    m = jnp.mean(x, axis=axis, keepdims=True)
    v = jnp.var(x, axis=axis, keepdims=True)
    return (x - m) / jnp.sqrt(v + eps)

def _scatter_add(tgt, idx, src, axis=0):
    return tgt.at[idx].add(src)

def _segment_sum(src, seg, n):
    return jax.ops.segment_sum(src, seg, n)
kernel_name = 'mk_decoder_preln_d1_seqx_r4_b50ccf'

def setup_inputs(seed: int=0):
    np.random.seed(seed)
    _w = jnp.asarray

    def _rec_inputs():
        import jax
        import jax.numpy as jnp
        _rk = jax.random.key(seed)
        x = 0.0003765 + 1 * jax.random.normal(jax.random.fold_in(_rk, 1), (8, 256, 256), jnp.float32)
        _lenS = 256 - jax.random.randint(jax.random.fold_in(_rk, 7), (8,), 0, max(1, 256 // 4) + 1, jnp.int32)
        _lenS2 = 256 - jax.random.randint(jax.random.fold_in(_rk, 8), (8,), 0, max(1, 256 // 4) + 1, jnp.int32)
        _ctx_1024P = jax.random.normal(jax.random.fold_in(_rk, 11), (8, 16, 256), jnp.float32)
        _ctx_1024c = jax.random.dirichlet(jax.random.fold_in(_rk, 511), 0.3 * jnp.ones((16,), jnp.float32), (8, 256))
        _ctx_1024t = jnp.einsum('bsk,bkd->bsd', _ctx_1024c, _ctx_1024P)
        _ctx_1024t = _ctx_1024t * jax.lax.rsqrt(jnp.mean(jnp.square(_ctx_1024t)) + 1e-12) * 0.953939
        ctx_1024 = -0.000292821 + 1.00034 * (_ctx_1024t + 0.3 * jax.random.normal(jax.random.fold_in(_rk, 611), (8, 256, 256), jnp.float32))
        _validS = jnp.arange(256)[None, :] < _lenS[:, None]
        _validS2 = jnp.arange(256)[None, :] < _lenS2[:, None]
        _causal = jnp.tril(jnp.ones((256, 256), dtype=bool))
        mask_1x1xSxS2_ik0 = jnp.where(jnp.broadcast_to(_validS2[0:1, None, None, :], (1, 1, 256, 256)), 0, 1).astype(jnp.int32)
        return (x, ctx_1024, mask_1x1xSxS2_ik0)
    x, ctx_1024, mask_1x1xSxS2_ik0 = _rec_inputs()

    def _L0_attn_setup():
        import jax, jax.numpy as jnp
        import numpy as np
        B, S, D = (4, 512, 256)
        GAMMA = 1.0
        key = jax.random.key(seed)
        ks = jax.random.split(key, 9)
        scale = 1.0 / np.sqrt(D)
        return {'x': jax.random.normal(ks[0], (B, S, D), dtype=jnp.float32), 'Wq': jax.random.normal(ks[1], (D, D), dtype=jnp.float32) * scale, 'bq': jax.random.normal(ks[2], (D,), dtype=jnp.float32) * 0.01, 'Wk': jax.random.normal(ks[3], (D, D), dtype=jnp.float32) * scale, 'bk': jax.random.normal(ks[4], (D,), dtype=jnp.float32) * 0.01, 'Wv': jax.random.normal(ks[5], (D, D), dtype=jnp.float32) * scale, 'bv': jax.random.normal(ks[6], (D,), dtype=jnp.float32) * 0.01, 'Wo': jax.random.normal(ks[7], (D, D), dtype=jnp.float32) * scale, 'bo': jax.random.normal(ks[8], (D,), dtype=jnp.float32) * 0.01}
    _L0_attn_all = _L0_attn_setup()
    _L0_attn_in = {k: v for k, v in _L0_attn_all.items() if k in ('Wq', 'bq', 'Wk', 'bk', 'Wv', 'bv', 'Wo', 'bo')}
    del _L0_attn_all

    def _L0_xattn_setup():
        import jax, jax.numpy as jnp
        import numpy as np
        HEADS = 16
        key = jax.random.key(seed)
        ks = jax.random.split(key, 8)
        N, S, E = (2, 512, 256)
        scale = 1.0 / np.sqrt(E)
        inp = {'values': jax.random.normal(ks[0], (N, S, E), jnp.float32), 'keys': jax.random.normal(ks[1], (N, S, E), jnp.float32), 'query': jax.random.normal(ks[2], (N, S, E), jnp.float32), 'mask': jnp.tril(jnp.ones((1, 1, S, S), jnp.int32)), 'Wv': jax.random.normal(ks[3], (E, E), jnp.float32) * scale, 'bv': jnp.zeros((E,), jnp.float32), 'Wk': jax.random.normal(ks[4], (E, E), jnp.float32) * scale, 'bk': jnp.zeros((E,), jnp.float32), 'Wq': jax.random.normal(ks[5], (E, E), jnp.float32) * scale, 'bq': jnp.zeros((E,), jnp.float32), 'Wo': jax.random.normal(ks[6], (E, E), jnp.float32) * scale, 'bo': jnp.zeros((E,), jnp.float32)}
        return inp
    _L0_xattn_all = _L0_xattn_setup()
    _L0_xattn_in = {k: v for k, v in _L0_xattn_all.items() if k in ('Wv', 'bv', 'Wk', 'bk', 'Wq', 'bq', 'Wo', 'bo')}
    del _L0_xattn_all

    def _L0_ffn_setup():
        import jax, jax.numpy as jnp
        import numpy as np
        D_MODEL, D_FF, N_EXPERTS, TOP_K = (256, 1024, 8, 2)
        key = jax.random.key(seed)
        k0, k1, k2, k3 = jax.random.split(key, 4)
        x = jax.random.normal(k0, (2, 512, D_MODEL), dtype=jnp.float32)
        Wg = jax.random.normal(k1, (D_MODEL, N_EXPERTS), dtype=jnp.float32) * 0.02
        W1 = jax.random.normal(k2, (N_EXPERTS, D_MODEL, D_FF), dtype=jnp.float32) * 0.02
        b1 = jnp.zeros((N_EXPERTS, D_FF), dtype=jnp.float32)
        W2 = jax.random.normal(k3, (N_EXPERTS, D_FF, D_MODEL), dtype=jnp.float32) * 0.02
        b2 = jnp.zeros((N_EXPERTS, D_MODEL), dtype=jnp.float32)
        return {'x': x, 'Wg': Wg, 'W1': W1, 'b1': b1, 'W2': W2, 'b2': b2}
    _L0_ffn_all = _L0_ffn_setup()
    _L0_ffn_in = {k: v for k, v in _L0_ffn_all.items() if k in ('Wg', 'W1', 'b1', 'W2', 'b2')}
    del _L0_ffn_all
    return {'x': x, 'ctx_1024': ctx_1024, 'mask_1x1xSxS2_ik0': mask_1x1xSxS2_ik0, 'L0_attn_Wq': _L0_attn_in['Wq'], 'L0_attn_bq': _L0_attn_in['bq'], 'L0_attn_Wk': _L0_attn_in['Wk'], 'L0_attn_bk': _L0_attn_in['bk'], 'L0_attn_Wv': _L0_attn_in['Wv'], 'L0_attn_bv': _L0_attn_in['bv'], 'L0_attn_Wo': _L0_attn_in['Wo'], 'L0_attn_bo': _L0_attn_in['bo'], 'L0_xattn_Wv': _L0_xattn_in['Wv'], 'L0_xattn_bv': _L0_xattn_in['bv'], 'L0_xattn_Wk': _L0_xattn_in['Wk'], 'L0_xattn_bk': _L0_xattn_in['bk'], 'L0_xattn_Wq': _L0_xattn_in['Wq'], 'L0_xattn_bq': _L0_xattn_in['bq'], 'L0_xattn_Wo': _L0_xattn_in['Wo'], 'L0_xattn_bo': _L0_xattn_in['bo'], 'L0_ffn_Wg': _L0_ffn_in['Wg'], 'L0_ffn_W1': _L0_ffn_in['W1'], 'L0_ffn_b1': _L0_ffn_in['b1'], 'L0_ffn_W2': _L0_ffn_in['W2'], 'L0_ffn_b2': _L0_ffn_in['b2']}

def reference(x, ctx_1024, mask_1x1xSxS2_ik0, L0_attn_Wq, L0_attn_bq, L0_attn_Wk, L0_attn_bk, L0_attn_Wv, L0_attn_bv, L0_attn_Wo, L0_attn_bo, L0_xattn_Wv, L0_xattn_bv, L0_xattn_Wk, L0_xattn_bk, L0_xattn_Wq, L0_xattn_bq, L0_xattn_Wo, L0_xattn_bo, L0_ffn_Wg, L0_ffn_W1, L0_ffn_b1, L0_ffn_W2, L0_ffn_b2):
    import jax
    import jax.numpy as jnp

    def _L0_attn_ref(x, Wq, bq, Wk, bk, Wv, bv, Wo, bo):
        import jax, jax.numpy as jnp
        import numpy as np
        B, S, D = (4, 512, 256)
        GAMMA = 1.0
        q = x @ Wq + bq
        k = x @ Wk + bk
        v = x @ Wv + bv
        q_sq = jnp.sum(q * q, axis=-1)
        k_sq = jnp.sum(k * k, axis=-1)
        qk = jnp.einsum('bqd,bkd->bqk', q, k)
        dist_sq = q_sq[:, :, None] + k_sq[:, None, :] - 2.0 * qk
        scores = jnp.exp(-GAMMA * dist_sq)
        attn = jax.nn.softmax(scores, axis=-1)
        out = jnp.einsum('bqk,bkd->bqd', attn, v)
        return out @ Wo + bo

    def _L0_xattn_ref(values, keys, query, mask, Wv, bv, Wk, bk, Wq, bq, Wo, bo):
        import jax, jax.numpy as jnp
        import numpy as np
        HEADS = 16
        N, Lq, E = query.shape
        H = HEADS
        D = E // H
        v = (values @ Wv + bv).reshape(N, -1, H, D)
        k = (keys @ Wk + bk).reshape(N, -1, H, D)
        q = (query @ Wq + bq).reshape(N, Lq, H, D)
        energy = jnp.einsum('nqhd,nkhd->nhqk', q, k)
        neg = jnp.finfo(energy.dtype).min
        energy = jnp.where(mask == 0, neg, energy)
        attn = jax.nn.softmax(energy / jnp.sqrt(jnp.asarray(D, energy.dtype)), axis=-1)
        out = jnp.einsum('nhqk,nkhd->nqhd', attn, v).reshape(N, Lq, E)
        return out @ Wo + bo

    def _L0_ffn_ref(x, Wg, W1, b1, W2, b2):
        import jax, jax.numpy as jnp
        import numpy as np
        D_MODEL, D_FF, N_EXPERTS, TOP_K = (256, 1024, 8, 2)
        B = x.shape[:-1]
        xs = x.reshape(-1, x.shape[-1])
        T = xs.shape[0]
        gate_logits = xs @ Wg
        weights, sel = jax.lax.top_k(gate_logits, TOP_K)
        weights = jax.nn.softmax(weights.astype(jnp.float32), axis=1).astype(x.dtype)
        h = jax.nn.relu(jnp.einsum('td,edf->etf', xs, W1) + b1[:, None, :])
        out_e = jnp.einsum('etf,efd->etd', h, W2) + b2[:, None, :]
        tok = jnp.arange(T)
        picked = out_e[sel, tok[:, None]]
        out = jnp.einsum('tk,tkd->td', weights, picked)
        return out.reshape(*B, x.shape[-1])
    x = x + _L0_attn_ref(_layernorm(x, axis=-1), L0_attn_Wq, L0_attn_bq, L0_attn_Wk, L0_attn_bk, L0_attn_Wv, L0_attn_bv, L0_attn_Wo, L0_attn_bo)
    x = x + _L0_xattn_ref(ctx_1024, ctx_1024, _layernorm(x, axis=-1), mask_1x1xSxS2_ik0, L0_xattn_Wv, L0_xattn_bv, L0_xattn_Wk, L0_xattn_bk, L0_xattn_Wq, L0_xattn_bq, L0_xattn_Wo, L0_xattn_bo)
    x = x + _L0_ffn_ref(_layernorm(x, axis=-1), L0_ffn_Wg, L0_ffn_W1, L0_ffn_b1, L0_ffn_W2, L0_ffn_b2)
    return x

_drawn_inputs = setup_inputs


def setup_inputs(seed=0):
    import zlib

    import numpy as np

    out = dict(_drawn_inputs(seed))
    spreads = {'L0_xattn_bv': (0.0, 0.1),
     'L0_xattn_bk': (0.0, 0.8),
     'L0_xattn_bq': (0.0, 0.269),
     'L0_xattn_bo': (0.0, 0.1),
     'L0_ffn_b1': (0.0, 0.293),
     'L0_ffn_b2': (0.0, 0.1)}
    factors = {'L0_attn_bv': 4.309, 'L0_attn_bo': 4.773}
    for name, (base, spread) in spreads.items():
        noise = np.random.default_rng([zlib.crc32(name.encode()), seed]).standard_normal(out[name].shape)
        drawn = base * np.exp(spread * noise) if base else spread * noise
        out[name] = jnp.asarray(drawn.astype(out[name].dtype))
    for name, factor in factors.items():
        out[name] = (out[name] * factor).astype(out[name].dtype)
    return out
```

```python
from contextlib import ExitStack
from functools import partial

import concourse.bass as bass
from concourse import mybir

F32 = mybir.dt.float32
F32R = mybir.dt.float32r
BF16 = mybir.dt.bfloat16
I32 = mybir.dt.int32
U32 = mybir.dt.uint32
ALU = mybir.AluOpType
ACT = mybir.ActivationFunctionType
AX = mybir.AxisListType

P = 128
NB = 8
S = 256
D = 256
KT = D // P
H = 16
HD = D // H
NE = 8
FF = 1024
FT = FF // P
TT = NB * S // P
EPS = 1e-5
MASKED = -(2.0 ** 120)
WEIGHTS = [(m, n) for m in ("attn", "xattn") for n in ("Wq", "Wk", "Wv", "Wo")]
ATT_LAG = 2
MOE_LAG = 4
MAX_TILES = (2 * NB * S + NE * (P - 1)) // P


class Step:

    def __init__(self, j, u):
        self.j, self.u = j, u
        self.v = 2 * j + u
        self.p = u

    def back(self, k):
        n = self.u - k
        return Step(self.j + n // 2, n % 2)

    def inside(self, count):
        return not isinstance(self.v, int) or 0 <= self.v < count


def pipeline(eng, count, lag, body, first=2, ahead=0):
    for n in range(-ahead, first):
        body(Step(n // 2, n % 2))
    pairs = (count - first - ahead) // 2
    with eng.Fori(first // 2, first // 2 + pairs) as j:
        for u in range(2):
            body(Step(j, u))
    for n in range(first + 2 * pairs, count + lag):
        body(Step(n // 2, n % 2))


def wait_count(eng, sem, count, apart):
    if apart is not None and not isinstance(count, int):
        register, passed = apart
        eng.reg_mov(register, count)
        count = eng.snap(register)
        eng.wait_ge(passed, 16)
    eng.wait_ge(sem, count)


class Event:

    def __init__(self, sem, per=1, unit=1):
        self.sem, self.per, self.unit = sem, per, unit

    def at(self, inst):
        inst.then_inc(self.sem, self.unit)

    def wait(self, eng, step, k=None, apart=None):
        if isinstance(step.v, int) and step.v < 0:
            return
        n = self.per if k is None else k + 1
        wait_count(eng, self.sem, step.j * (2 * self.per * self.unit) + (step.u * self.per + n) * self.unit, apart)


class ParityDma:

    def __init__(self, sems, per=1):
        self.sems, self.per = sems, per

    def at(self, inst, step):
        inst.then_inc(self.sems[step.p], 16)

    def wait(self, eng, step, apart=None):
        if isinstance(step.v, int) and step.v < 0:
            return
        wait_count(eng, self.sems[step.p], step.j * (16 * self.per) + 16 * self.per, apart)


def build(nc, inputs, out):
    with ExitStack() as ctx:
        run(Core(nc, inputs, out, ctx))


class Core:

    def __init__(self, nc, t, out, ctx):
        self.nc, self.t, self.out, self.ctx = nc, t, out, ctx
        self.e, self.m, self.hi, self.lo = {}, {}, {}, {}
        self.xn_dram = nc.dram_tensor("xn_rows", (NB * S, D), F32).ap()
        self.choice_dram = nc.dram_tensor("choice_rows_dram", (2 * NB * S, D), F32).ap()


def sem(core, name):
    return core.ctx.enter_context(core.nc.semaphore(name))


def event(core, name, per=1):
    return Event(sem(core, name), per)


def dma_event(core, name, per=1):
    return ParityDma([sem(core, f"{name}{i}") for i in range(2)], per)


def run(core):
    nc, t = core.nc, core.t
    core.psum = [core.ctx.enter_context(nc.psum_tensor(f"bank{i}", [P, 512], F32)) for i in range(8)]
    top = nc.sbuf_usable_end
    core.base = (nc.sbuf_base + 63) // 64 * 64
    core.cursor = core.base
    core.top = top
    plan_shared(core)
    shared_end = core.cursor
    plan_attention(core)
    core.cursor = shared_end
    plan_experts(core)
    make_events(core)
    block = core.ctx.enter_context(nc.Block())
    programs = {
        "sync": (block.sync, setup_sync, routing_sync, finish_sync),
        "gpsimd": (block.gpsimd, setup_gpsimd, routing_gpsimd, finish_gpsimd),
        "scalar": (block.scalar, setup_scalar, routing_scalar, finish_scalar),
        "tensor": (block.tensor, setup_tensor, routing_tensor, finish_tensor),
        "vector": (block.vector, setup_vector, routing_vector, finish_vector),
    }
    for name, (engine, setup, routing, finish) in programs.items():
        @engine
        def _(eng, name=name, setup=setup, routing=routing, finish=finish):
            core.apart = (eng.alloc_register(f"{name}_count"), core.E["x_first0"])
            setup(core, eng)
            pipeline(eng, NB, ATT_LAG, lambda it: attention(core, name, eng, it), ahead=1)
            attention_over(core, eng)
            routing(core, eng)
            pipeline(eng, MAX_TILES, MOE_LAG, lambda it: experts(core, name, eng, it), first=6)
            finish(core, eng)


def buffer(core, name, free, dt=F32, parts=P):
    size = {F32: 4, F32R: 4, BF16: 2, I32: 4, U32: 4}[dt]
    n = 1
    for f in free:
        n *= f
    handle = core.nc.alloc_sbuf_tensor_at(name, [parts, *free], dt, offset=core.cursor, align_bytes=32)
    core.cursor += (n * size + 31) // 32 * 32
    assert core.cursor <= core.top, (name, core.cursor, core.top)
    return handle


def plan_shared(core):
    core.ident = buffer(core, "ident", [P])
    core.ones = buffer(core, "ones", [P])
    core.x2 = buffer(core, "x2", [TT, D])
    core.logits = buffer(core, "logits", [TT, NE])
    core.gate_w = buffer(core, "gate_w", [KT, NE])
    core.tile_expert = buffer(core, "tile_expert", [MAX_TILES + 1], I32)
    core.gather_idx = buffer(core, "gather_idx", [MAX_TILES], U32)
    core.scatter_idx = buffer(core, "scatter_idx", [MAX_TILES], U32)
    core.slot_weight = buffer(core, "slot_weight", [MAX_TILES])


def plan_attention(core):
    sb = partial(buffer, core)
    core.ident_bf = sb("ident_bf", [P], BF16)
    core.neg_half = sb("neg_half", [P])
    core.ctx_in = sb("ctx_in", [KT, D])
    core.xn = sb("xn", [KT, D])
    core.xn_cross = sb("xn_cross", [KT, D])
    core.xn_ffn = sb("xn_ffn", [KT, D])
    core.x1 = sb("x1", [KT, D])
    core.tr_hi = [sb(f"tr_hi{i}", [KT, S], F32R) for i in range(2)]
    core.tr_lo = [sb(f"tr_lo{i}", [KT, S], F32R) for i in range(2)]
    core.full = [sb(f"full{i}", [KT, S]) for i in range(3)]
    for n in ("q", "k", "v", "cq", "ck", "p"):
        core.hi[n] = sb(n + "_hi", [KT, S], F32R)
        core.lo[n] = sb(n + "_lo", [KT, S], F32R)
    core.q_sq, core.k_sq = sb("q_sq", [KT, S]), sb("k_sq", [KT, S])
    core.prob = sb("prob", [KT, S])
    core.q_stack = sb("q_stack", [H, S], F32R)
    core.k_stack = sb("k_stack", [H, S], F32R)
    core.v_aug = [sb(f"v_aug{i}", [KT, H, 32]) for i in range(2)]
    core.exp_ring = sb("exp_ring", [8, 2, S])
    core.heads_t = sb("heads_t", [4, S])
    core.heads = sb("heads", [KT, D])
    core.w = {}
    for n in ("Wq", "Wk", "Wv", "Wo"):
        for m in ("attn", "xattn"):
            core.w[m, n] = (sb(f"{m}{n}h", [KT, D], F32R), sb(f"{m}{n}l", [KT, D], F32R))
    core.bias_row = {k: sb("bias_" + "_".join(k), [D])
                     for k in (("attn", "bv"), ("attn", "bo"), ("xattn", "bv"), ("xattn", "bo"))}
    core.bias_col = {k: sb("bias_" + "_".join(k), [KT])
                     for k in (("attn", "bq"), ("attn", "bk"), ("xattn", "bq"), ("xattn", "bk"))}
    core.mask_q = sb("mask_q", [KT, S], BF16)
    core.mask_k = sb("mask_k", [KT, S], BF16)
    core.stats = sb("stats", [3, KT, 6])
    core.moments = sb("moments", [3, KT, 2])
    core.rstd = sb("rstd", [3, KT])
    core.minus_half = sb("minus_half", [KT])
    core.neg_ksq = sb("neg_ksq", [KT])
    core.r_den = sb("r_den", [KT])
    core.neg_max = sb("neg_max", [KT, H])
    core.max_hi = sb("max_hi", [S], F32R)
    core.max_lo = sb("max_lo", [S], F32R)
    core.r_heads = sb("r_heads", [KT, H])
    core.one_rows = sb("one_rows", [S], F32R, parts=1)
    core.mask_int = core.full[0][:, :, :].bitcast(I32)


def plan_experts(core):
    sb = partial(buffer, core)
    core.w1_offset = core.cursor
    core.w1 = sb("w1", [NE * KT * FF])
    core.w2 = sb("w2", [NE * FT * D])
    core.b1_rows = sb("b1_rows", [P])
    core.b1_cols = sb("b1_cols", [NE * FT])
    core.b2_row = sb("b2_row", [NE * D])
    core.slots_in = [sb(f"slots_in{i}", [D]) for i in range(2)]
    core.slots_t = [sb(f"slots_t{i}", [KT, P]) for i in range(2)]
    core.hid = [sb(f"hid{i}", [FF]) for i in range(2)]
    core.hid_t = [sb(f"hid_t{i}", [FT, P]) for i in range(2)]
    core.y = [sb(f"y{i}", [D]) for i in range(2)]
    core.b1_tile = [sb(f"b1_tile{i}", [FT]) for i in range(2)]
    after = core.cursor
    core.gather_now = [sb(f"gather_now{i}", [1], U32) for i in range(2)]
    core.scatter_now = [sb(f"scatter_now{i}", [1], U32) for i in range(2)]
    core.top8 = sb("top8", [TT, 8])
    core.idx8 = sb("idx8", [TT, 8], U32)
    core.choice = sb("choice", [TT, 2])
    core.onehot = sb("onehot", [2, TT, NE])
    core.both = sb("both", [TT, NE])
    core.running = [sb(f"running{i}", [TT, NE]) for i in range(2)]
    core.slot_of = sb("slot_of", [TT, NE])
    core.picked = sb("picked", [TT, NE])
    core.slot = sb("slot", [2, TT])
    core.counts = sb("counts", [NE])
    core.cmp16 = sb("cmp16", [NE, 16])
    core.tiles_of = [sb(f"tiles_of{i}", [NE]) for i in range(2)]
    core.first_slot = sb("first_slot", [NE])
    core.cmp_tiles = sb("cmp_tiles", [MAX_TILES + 1, NE - 1])
    core.expert_f = sb("expert_f", [MAX_TILES + 1])
    core.iota_i = sb("iota_i", [P], I32)
    core.iota_f = sb("iota_f", [P])
    core.iota_p = sb("iota_p", [TT], I32)
    core.token_f = sb("token_f", [2, TT])
    core.strict = sb("strict", [P])
    core.delta = sb("delta", [TT])
    core.ex = sb("ex", [TT])
    core.one_plus = sb("one_plus", [TT])
    core.weight = sb("weight", [2, TT])
    core.slot_tile = sb("slot_tile", [2, TT])
    core.slot_row = sb("slot_row", [2, TT])
    core.cmp_slots = sb("cmp_slots", [2 * TT, MAX_TILES])
    core.own_tiles = sb("own_tiles", [NE])
    core.row_hot = [sb(f"row_hot{i}", [P]) for i in range(2)]
    core.tile_vals = [sb(f"tile_vals{i}", [2, MAX_TILES]) for i in range(2)]
    core.slot_id = sb("slot_id", [MAX_TILES])
    core.slot_tmp = sb("slot_tmp", [4, MAX_TILES])
    core.cursor = core.w1_offset
    core.choice_rows = [sb(f"choice_rows{i}", [2, 4, D]) for i in range(2)]


def make_events(core):
    ev = partial(event, core)
    dma = partial(dma_event, core)
    E = core.E = {}
    for n in "x_first0 x_first1 x_rest consts_in weights bias_rows mask_in experts_w1 experts_w2 experts_b".split():
        E[n] = sem(core, n)
    for n in "const_pool const_vec weights_split masks_ready neg_mask prior_pool".split():
        E[n] = sem(core, n)
    core.ctx_loaded = dma("ctx_loaded")
    core.q_stacked, core.k_stacked = dma("q_stacked", 6), dma("k_stacked", 6)
    core.m["stacked"] = dma("m_stacked", 2)
    core.xn_stored = dma("xn_stored")
    per = dict(
        ln0_stats=4, ln0_eps=1, ln0_rstd=1, ln0=2, ln1_stats=4, ln1_eps=1, ln1_rstd=1, ln1=2,
        ln2_stats=4, ln2_eps=1, ln2_rstd=1, ln2=2,
        xb=1, resid1=1,
        p_xnT=1, p_q=1, p_k=1, p_v=1, p_ksq=1, p_s1=1, p_o=1, p_den=1, p_y=1, p_xcT=1, p_cq=1,
        p_ctxT=1, p_ck=1, p_cv=1, p_max=1, p_headsT=2, p_hT=1, p_y2=1, p_xfT=1, p_gate=1,
        s_tile=16, t_tile=16, av=4,
        xnT_hi=1, xnT_lo=1, q_hi=2, k_hi=2, v_full=1, q_square=2, k_square=2,
        q_split=2, k_split=2, v_hi=1, v_split=1, ksq=1, e1=2, e2=1, p_hi=1, p_split=1, oT_hi=1, oT_lo=1, den=1, x1=2,
        xcT_hi=1, xcT_lo=1, cq_hi=2, cq_split=2, ctxT_hi=1, ctxT_lo=1, ck_hi=2, ck_split=2,
        cv=2, maxed=16, m_hi=1, m_lo=1, exp=16, av_out=2, r_heads=2, headsN=2, hT_hi=1, hT_lo=1,
        x2=1, xfT=1, gate=1,
    )
    for n, k in per.items():
        core.e[n] = ev("e_" + n, k)
    core.r = {n: sem(core, "r_" + n) for n in
              "vec pool act both prefix delta ex hot0 hot1 slots table idx b1_in b1_t b1_cols".split()}
    core.rows_in, core.rows_out = dma_event(core, "rows_in"), dma_event(core, "rows_out")
    per = dict(gnow=1, snow=1, xT=1, slots_t=1, hid=2, hid_a=1, hid_v=1, hidT=2, act_a=4, act_v=4, b1t=1,
               out=1, y=2)
    for n, k in per.items():
        core.m[n] = ev("m_" + n, k)
    core.choice_in, core.sums, core.stored = dma_event(core, "choice_in"), sem(core, "sums"), sem(core, "stored")


def loads(core, eng, dst, src, sem):
    eng.dma_start(dst, src).then_inc(sem, 16)


def x2_of(core, b):
    return core.x2[:, bass.ds(b.v * KT, KT), :]


def setup_sync(core, e):
    t, E = core.t, core.E
    x_rows = t["x"].rearrange("b (t p) d -> p (b t) d", p=P)
    for b in range(2):
        loads(core, e, core.x2[:, b * KT:(b + 1) * KT, :], x_rows[:, b * KT:(b + 1) * KT, :], E[f"x_first{b}"])
    for i, (m, n) in enumerate(WEIGHTS):
        loads(core, e, raw_weight(core, i), t[f"L0_{m}_{n}"].rearrange("(k p) n -> p k n", p=P), E["weights"])
    loads(core, e, core.x2[:, 2 * KT:, :], x_rows[:, 2 * KT:, :], E["x_rest"])


def raw_weight(core, i):
    return core.exp_ring[:, i, :, :]


def weight_pieces(core):
    pieces = []
    for i, key in enumerate(WEIGHTS):
        raw, (hi, lo) = raw_weight(core, i), core.w[key]
        if key in (("xattn", "Wq"), ("xattn", "Wk")):
            for k in range(KT):
                pieces.append((raw[:, k, :].rearrange("p (c h d) -> p c d h", c=KT, d=HD),
                               *(w[:, k, :].rearrange("p (c d h) -> p c d h", c=KT, d=HD) for w in (hi, lo))))
        else:
            pieces.append((raw, hi[:, :, :], lo[:, :, :]))
    return pieces


def setup_scalar(core, e):
    t, E = core.t, core.E
    mask = t["mask_1x1xSxS2_ik0"].rearrange("a b q k -> (a b q) k")
    loads(core, e, core.mask_int, mask.rearrange("(t p) k -> p t k", p=P), E["mask_in"])
    for (m, n), dst in core.bias_col.items():
        with core.nc.allow_non_contiguous_dma("256 bias values, one per partition"):
            for k in range(KT):
                col = t[f"L0_{m}_{n}"][k * P:(k + 1) * P]
                col = (col.rearrange("(h d o) -> d h o", d=HD, o=1) if m == "xattn"
                       else col.rearrange("(p o) -> p o", o=1))
                loads(core, e, dst[:, k:k + 1], col, E["consts_in"])
    for (m, n), dst in core.bias_row.items():
        row = t[f"L0_{m}_{n}"].rearrange("(a n) -> a n", a=1)
        loads(core, e, dst[:, :], row.partition_broadcast(P), E["consts_in"])
    loads(core, e, core.gate_w[:, :, :], t["L0_ffn_Wg"].rearrange("(k p) n -> p k n", p=P), E["consts_in"])
    e.wait_ge(E["weights"], 16 * len(WEIGHTS))
    for raw, hi, lo in weight_pieces(core):
        e.activation(hi, raw, ACT.Copy).then_inc(E["weights_split"], 1)
    e.wait_ge(E["neg_mask"], 2)
    e.activation(core.mask_k[:, :, :], core.psum[7][:, :], ACT.Copy).then_inc(E["masks_ready"], 1)


def setup_gpsimd(core, e):
    E, pool = core.E, core.E["const_pool"]
    e.memset(core.ident[:, :], 0.0).then_inc(pool, 1)
    e.wait_ge(pool, 1)
    e.affine_select(out=core.ident[:, :], in_=core.ident[:, :], compare_op=ALU.not_equal, fill=1.0,
                    base=0, pattern=[[-1, P]], channel_multiplier=1).then_inc(pool, 1)
    e.memset(core.ones[:, :], 1.0).then_inc(pool, 1)
    e.memset(core.neg_half[:, :], -0.5).then_inc(pool, 1)
    e.memset(core.minus_half[:, :], -0.5).then_inc(pool, 1)
    e.wait_ge(pool, 2)
    e.tensor_copy(core.ident_bf[:, :], core.ident[:, :]).then_inc(pool, 1)
    for i in range(2):
        e.memset(core.v_aug[i][:, :, :, :], 0.0).then_inc(pool, 1)
    e.wait_ge(pool, 8)
    for i in range(2):
        e.memset(core.v_aug[i][:, :, :, HD:HD + 1], 1.0).then_inc(pool, 1)
    e.wait_ge(pool, 3)
    e.tensor_copy(core.one_rows[:, :], core.ones[0:1, 0:1].to_broadcast([1, S])).then_inc(pool, 1)
    e.wait_ge(pool, 11)
    for p in range(2):
        for r in range(2):
            row = 64 * p + 3 * HD + r
            e.dma_start(core.k_stack[row:row + 1, :, :].bitcast(F32),
                        core.one_rows[0:1, :].bitcast(F32).rearrange("a (o s) -> a o s", o=1).to_broadcast([1, H, S])
                        ).then_inc(E["prior_pool"], 16)


def setup_vector(core, e):
    E = core.E
    e.wait_ge(E["mask_in"], 16)
    e.tensor_scalar(core.mask_q[:, :, :], core.mask_int, 0.0, MASKED, ALU.is_equal, ALU.mult)\
        .then_inc(E["neg_mask"], 1)
    for i, (raw, hi, lo) in enumerate(weight_pieces(core)):
        e.wait_ge(E["weights_split"], i + 1)
        e.tensor_tensor(lo, raw, hi.bitcast(F32), ALU.subtract).then_inc(E["const_vec"], 1)


def setup_tensor(core, e):
    E = core.E
    e.wait_ge(E["const_pool"], 11)
    e.wait_ge(E["neg_mask"], 1)
    for kt in range(KT):
        for qt in range(KT):
            mm = e.matmul(core.psum[7][:, kt * S + qt * P:kt * S + (qt + 1) * P],
                          core.mask_q[:, qt, kt * P:(kt + 1) * P], core.ident_bf[:, :], start=True, stop=True)
    mm.then_inc(E["neg_mask"], 1)
    e.wait_ge(E["const_vec"], len(weight_pieces(core)))
    e.wait_ge(E["prior_pool"], 64)
    e.wait_ge(E["masks_ready"], 1)
    e.wait_ge(E["consts_in"], 16 * 13)


def attention(core, name, eng, it):
    def at(lag, fn, *args):
        b = it.back(lag)
        if b.inside(NB):
            fn(core, name, eng, b, it, *args)

    at(0, st_transpose, "xnT")
    at(1, st_scores, 0)
    at(0, st_project, "q")
    at(1, st_scores, 1)
    at(0, st_project, "k")
    at(1, st_scores, 2)
    at(0, st_value)
    at(2, st_heads_transposed)
    at(1, st_scores, 3)
    at(0, st_key_norms)
    at(0, st_rbf)
    at(2, st_transpose, "hT")
    at(1, st_scores, 4)
    at(0, st_rbf_split)
    at(2, st_output)
    at(1, st_scores, 5)
    at(2, st_ln, 2)
    at(0, st_rbf_out)
    at(1, st_scores, 6)
    at(0, st_transpose, "ctxT")
    at(1, st_scores, 7)
    at(0, st_self_output)
    at(1, st_maxima)
    at(0, st_project, "ck")
    at(0, st_ln, 1)
    at(0, st_cross_value)
    at(2, st_router_transpose)
    at(2, st_router)
    at(0, st_transpose, "xcT")
    at(1, st_exps, 0)
    at(0, st_project, "cq")
    at(1, st_exps, 1)
    at(1, st_exps, 2)
    at(1, st_weighted, 0)
    at(1, st_exps, 3)
    at(-1, st_ln, 0)
    at(1, st_exps, 4)
    at(1, st_weighted, 1)
    at(1, st_exps, 5)
    at(1, st_exps, 6)
    at(1, st_weighted, 2)
    at(1, st_exps, 7)
    at(1, st_weighted, 3)


def st_ln(core, name, eng, b, it, n):
    stats, eps_done, rstd_done, done = (core.e[f"ln{n}{x}"] for x in ("_stats", "_eps", "_rstd", ""))
    src = (x2_of(core, b), core.x1[:, :, :], x2_of(core, b))[n]
    if name == "vector":
        if n == 0:
            if isinstance(b.v, int) and b.v < 2:
                eng.wait_ge(core.E[f"x_first{b.v}"], 16)
            else:
                eng.wait_ge(core.E["x_rest"], 16)
        else:
            (core.e["x1"] if n == 1 else core.e["x2"]).wait(eng, b, apart=core.apart)
        for t in range(KT):
            stats.at(eng.bn_stats(core.stats[:, n, t, :], src[:, t, :]))
        for t in range(KT):
            stats.wait(eng, b, t, apart=core.apart)
            stats.at(eng.bn_aggr(core.moments[:, n, t, :], core.stats[:, n, t, :]))
        dst = (core.xn, core.xn_cross, core.xn_ffn)[n]
        rstd_done.wait(eng, b)
        if n == 2:
            core.e["p_xfT"].wait(eng, b.back(1))
            core.xn_stored.wait(eng, b.back(1))
        else:
            (core.e["p_xnT"], core.e["p_xcT"])[n].wait(eng, b.back(1))
        for t in range(KT):
            done.at(eng.tensor_scalar(dst[:, t, :], src[:, t, :], core.moments[:, n, t, 0:1],
                                      core.rstd[:, n, t:t + 1], ALU.subtract, ALU.mult))
    elif name == "gpsimd":
        stats.wait(eng, b, apart=core.apart)
        eps_done.at(eng.tensor_scalar(core.rstd[:, n, :], core.moments[:, n, :, 1], EPS, None, ALU.add))
        eps_done.wait(eng, b)
        rstd_done.at(eng.tensor_tensor(core.rstd[:, n, :], core.rstd[:, n, :], core.minus_half[:, :], ALU.pow))
        if n == 0:
            bias = core.bias_row["attn", "bo"][:, :].rearrange("p (o n) -> p o n", o=1).to_broadcast([P, KT, D])
            eng.wait_ge(core.E["consts_in"], 16 * 13)
            done.wait(eng, b)
            core.e["xb"].at(eng.tensor_tensor(x2_of(core, b), x2_of(core, b), bias, ALU.add))
    elif name == "sync":
        if n == 0:
            core.e["p_ctxT"].wait(eng, b.back(1), apart=core.apart)
            rows = core.t["ctx_1024"].rearrange("b (t p) d -> b p t d", p=P)
            core.ctx_loaded.at(eng.dma_start(core.ctx_in[:, :, :], rows[b.v]), b)
        if n == 2:
            done.wait(eng, b, apart=core.apart)
            rows = core.xn_dram.rearrange("(b t p) d -> b p t d", p=P, t=KT)
            core.xn_stored.at(eng.dma_start(rows[b.v], core.xn_ffn[:, :, :]), b)


def st_transpose(core, name, eng, b, it, which):
    src, bank, res = {
        "xnT": (core.xn, 2, 0), "hT": (core.heads, 1, 1),
        "ctxT": (core.ctx_in, 2, 1), "xcT": (core.xn_cross, 1, 0),
    }[which]
    done, hi, lo = (core.e[x] for x in (f"p_{which}", f"{which}_hi", f"{which}_lo"))
    ps = core.psum[bank]
    if name == "tensor":
        if which == "xnT":
            if b.back(3).inside(NB):
                core.e["gate"].wait(eng, b.back(3), 0)
            else:
                core.e["ck_split"].wait(eng, b.back(1), 1)
        elif which == "hT":
            core.e["headsN"].wait(eng, b, 1)
        elif which == "ctxT":
            if b.back(2).inside(NB):
                core.e["x2"].wait(eng, b.back(2), 0)
            else:
                core.e["ksq"].wait(eng, b, 0)
        elif which == "xcT":
            core.e["cv"].wait(eng, b, 1)
        if which == "ctxT":
            core.ctx_loaded.wait(eng, b)
        else:
            {"xnT": core.e["ln0"], "hT": core.e["headsN"], "xcT": core.e["ln1"]}[which].wait(eng, b)
        for c in range(KT):
            for t in range(KT):
                mm = eng.transpose(ps[:, c * S + t * P:c * S + (t + 1) * P], src[:, t, c * P:(c + 1) * P],
                                   core.ident[:, :])
        done.at(mm)
    elif name == "scalar":
        done.wait(eng, b)
        if which == "xnT":
            core.e["p_cq"].wait(eng, b.back(1), 0)
        elif which == "hT":
            if b.back(-1).inside(NB):
                core.e["p_cv"].wait(eng, b.back(-1), 0)
            else:
                core.e["p_y2"].wait(eng, b.back(1), 0)
        elif which == "ctxT":
            if b.back(2).inside(NB):
                core.e["p_y2"].wait(eng, b.back(2), 0)
            else:
                core.e["p_cv"].wait(eng, b.back(1), 0)
        elif which == "xcT":
            core.e["p_y"].wait(eng, b, 0)
        hi.at(eng.activation(core.tr_hi[res][:, :, :], ps[:, :], ACT.Copy))
    elif name == "vector":
        hi.wait(eng, b)
        if which == "xnT":
            core.e["p_cq"].wait(eng, b.back(1), 0)
        elif which == "hT":
            if b.back(-1).inside(NB):
                core.e["p_cv"].wait(eng, b.back(-1), 0)
            else:
                core.e["p_y2"].wait(eng, b.back(1), 0)
        elif which == "ctxT":
            if b.back(2).inside(NB):
                core.e["p_y2"].wait(eng, b.back(2), 0)
            else:
                core.e["p_cv"].wait(eng, b.back(1), 0)
        elif which == "xcT":
            core.e["p_y"].wait(eng, b, 0)
        lo.at(eng.tensor_tensor(core.tr_lo[res][:, :, :], ps[:, :], core.tr_hi[res][:, :, :].bitcast(F32),
                                ALU.subtract))


def split_product(eng, out, left, right, skip=False, start=True, stop=True):
    terms = [(lh, rh) for (lh, _), (rh, _) in zip(left, right)]
    terms += [(lh, rl) for (lh, _), (_, rl) in zip(left, right)]
    terms += [(ll, rh) for (_, ll), (rh, _) in zip(left, right)]
    for i, (a, b) in enumerate(terms):
        mm = eng.matmul(out, a, b, start=start and i == 0, stop=stop and i == len(terms) - 1,
                        skip_group_check=skip)
    return mm


def st_project(core, name, eng, b, it, which):
    m, n, bank, tr = {
        "q": ("attn", "q", 0, 0), "k": ("attn", "k", 1, 0),
        "ck": ("xattn", "k", 2, 1), "cq": ("xattn", "q", 0, 0),
    }[which]
    hi, lo = core.hi[which], core.lo[which]
    done, rounded, split = (core.e[x] for x in (f"p_{which}", f"{which}_hi", f"{which}_split"))
    bias = core.bias_col[m, "b" + n]
    source = {"q": core.e["xnT_lo"], "k": core.e["xnT_lo"], "ck": core.e["ctxT_lo"], "cq": core.e["xcT_lo"]}[which]
    ps = core.psum[bank]
    if name == "tensor":
        if which == "q":
            core.e["cq_split"].wait(eng, b.back(1), 1)
        elif which == "k":
            core.e["xcT_lo"].wait(eng, b.back(1), 0)
        elif which == "cq":
            if b.back(2).inside(NB):
                core.e["xfT"].wait(eng, b.back(2), 0)
            elif b.back(1).inside(NB):
                core.e["m_lo"].wait(eng, b.back(1), 0)
            else:
                core.e["den"].wait(eng, b, 0)
        elif which == "ck":
            core.e["ctxT_lo"].wait(eng, b, 0)
        source.wait(eng, b)
        w_hi, w_lo = core.w[m, "W" + n]
        for c in range(KT):
            mm = split_product(
                eng, ps[:, c * S:(c + 1) * S],
                [(w_hi[:, k, c * P:(c + 1) * P], w_lo[:, k, c * P:(c + 1) * P]) for k in range(KT)],
                [(core.tr_hi[tr][:, k, :], core.tr_lo[tr][:, k, :]) for k in range(KT)])
        done.at(mm)
    elif name == "scalar":
        done.wait(eng, b)
        if which in ("q", "k"):
            core.e["p_s1"].wait(eng, b.back(1))
        elif which == "cq":
            core.q_stacked.wait(eng, b.back(1))
        else:
            core.k_stacked.wait(eng, b.back(1))
        for c in range(KT):
            rounded.at(eng.activation(hi[:, c, :], ps[:, c * S:(c + 1) * S], ACT.Identity,
                                      bias=bias[:, c:c + 1]))
        if which in ("q", "k"):
            if which == "k":
                core.e["p_ksq"].wait(eng, b.back(1))
            dst_sq, ev = (core.q_sq, core.e["q_square"]) if which == "q" else (core.k_sq, core.e["k_square"])
            for c in range(KT):
                ev.at(eng.activation(dst_sq[:, c, :], ps[:, c * S:(c + 1) * S], ACT.Square, bias=bias[:, c:c + 1]))
    elif name == "vector":
        if which == "q":
            core.e["q_square"].wait(eng, b)
        elif which == "k":
            core.e["k_square"].wait(eng, b)
        else:
            rounded.wait(eng, b)
        for c in range(KT):
            split.at(eng.scalar_tensor_tensor(lo[:, c, :], ps[:, c * S:(c + 1) * S], bias[:, c:c + 1],
                                              hi[:, c, :].bitcast(F32), ALU.add, ALU.subtract))
    elif name == "sync" and which in ("ck", "cq"):
        stack, parts, ev = ((core.q_stack, (hi, hi, lo), core.q_stacked) if which == "cq"
                            else (core.k_stack, (hi, lo, hi), core.k_stacked))
        split.wait(eng, b, apart=core.apart)
        core.e["t_tile"].wait(eng, b.back(2), apart=core.apart)
        for r, part in enumerate(parts):
            for c in range(KT):
                rows = slice(64 * b.p + r * HD, 64 * b.p + (r + 1) * HD)
                h = H // KT
                ev.at(eng.dma_start(stack[rows, c * h:(c + 1) * h, :].bitcast(F32),
                                    part[:, c, :].bitcast(F32)), b)


def st_value(core, name, eng, b, it):
    ps = core.psum[2]
    if name == "tensor":
        core.e["xnT_lo"].wait(eng, b, 0)
        w_hi, w_lo = core.w["attn", "Wv"]
        for t in range(KT):
            mm = split_product(
                eng, ps[:, t * D:(t + 1) * D],
                [(core.tr_hi[0][:, k, t * P:(t + 1) * P], core.tr_lo[0][:, k, t * P:(t + 1) * P]) for k in range(KT)],
                [(w_hi[:, k, :], w_lo[:, k, :]) for k in range(KT)])
        core.e["p_v"].at(mm)
    elif name == "vector":
        core.e["p_v"].wait(eng, b)
        core.e["v_split"].wait(eng, b.back(1))
        bias = core.bias_row["attn", "bv"][:, :].rearrange("p (o n) -> p o n", o=1).to_broadcast([P, KT, D])
        core.e["v_full"].at(eng.tensor_tensor(core.full[0][:, :, :], ps[:, :].rearrange("p (t n) -> p t n", t=KT),
                                           bias, ALU.add))
    elif name == "scalar":
        core.e["v_full"].wait(eng, b)
        core.e["p_o"].wait(eng, b.back(1))
        core.e["v_hi"].at(eng.activation(core.hi["v"][:, :, :], core.full[0][:, :, :], ACT.Copy))
    elif name == "gpsimd":
        core.e["v_hi"].wait(eng, b)
        core.e["v_split"].at(eng.tensor_tensor(core.lo["v"][:, :, :], core.full[0][:, :, :],
                                               core.hi["v"][:, :, :].bitcast(F32), ALU.subtract))


def st_key_norms(core, name, eng, b, it):
    ps = core.psum[2]
    if name == "tensor":
        core.e["v_full"].wait(eng, b, 0)
        core.e["k_square"].wait(eng, b)
        for kt in range(KT):
            for c in range(KT):
                mm = eng.matmul(ps[:, kt:kt + 1], core.k_sq[:, c, kt * P:(kt + 1) * P], core.ones[:, 0:1],
                                start=c == 0, stop=c == KT - 1)
        core.e["p_ksq"].at(mm)
    elif name == "vector":
        core.e["p_ksq"].wait(eng, b)
        core.e["e1"].wait(eng, b.back(1))
        core.e["ksq"].at(eng.tensor_scalar(core.neg_ksq[:, :], ps[:, 0:KT], -1.0, None, ALU.mult))


def st_rbf(core, name, eng, b, it):
    ps = core.psum[0]
    if name == "tensor":
        if b.back(2).inside(NB):
            core.e["headsN"].wait(eng, b.back(2), 0)
        else:
            core.e["q_square"].wait(eng, b, 1)
            core.e["q_split"].wait(eng, b, 1)
        core.e["q_split"].wait(eng, b)
        core.e["k_split"].wait(eng, b)
        core.e["q_square"].wait(eng, b)
        for kt in range(KT):
            out = ps[:, kt * S:(kt + 1) * S]
            for c in range(KT):
                eng.matmul(out, core.neg_half[:, :], core.q_sq[:, c, :], start=c == 0, stop=False)
            rows = slice(kt * P, (kt + 1) * P)
            mm = split_product(
                eng, out, [(core.hi["k"][:, c, rows], core.lo["k"][:, c, rows]) for c in range(KT)],
                [(core.hi["q"][:, c, :], core.lo["q"][:, c, :]) for c in range(KT)], start=False)
        core.e["p_s1"].at(mm)
    elif name == "scalar":
        core.e["p_s1"].wait(eng, b)
        core.e["ksq"].wait(eng, b)
        core.e["e2"].wait(eng, b.back(1))
        for kt in range(KT):
            core.e["e1"].at(eng.activation(core.full[2][:, kt, :], ps[:, kt * S:(kt + 1) * S], ACT.Exp,
                                        bias=core.neg_ksq[:, kt:kt + 1], scale=2.0))
        core.e["e1"].wait(eng, b)
        core.e["p_den"].wait(eng, b.back(1))
        core.e["p_split"].wait(eng, b.back(1))
        core.e["e2"].at(eng.activation(core.prob[:, :, :], core.full[2][:, :, :], ACT.Exp))
        core.e["e2"].wait(eng, b)
        core.e["p_o"].wait(eng, b.back(1))
        core.e["p_hi"].at(eng.activation(core.hi["p"][:, :, :], core.prob[:, :, :], ACT.Copy))


def st_rbf_split(core, name, eng, b, it):
    if name == "vector":
        core.e["p_hi"].wait(eng, b)
        core.e["p_split"].at(eng.tensor_tensor(core.lo["p"][:, :, :], core.prob[:, :, :],
                                               core.hi["p"][:, :, :].bitcast(F32), ALU.subtract))


def st_rbf_out(core, name, eng, b, it):
    ps, den = core.psum[1], core.psum[0]
    if name == "tensor":
        if b.back(2).inside(NB):
            core.e["hT_lo"].wait(eng, b.back(2), 0)
        else:
            core.e["k_square"].wait(eng, b, 1)
            core.e["k_split"].wait(eng, b, 1)
        core.e["v_split"].wait(eng, b)
        core.e["p_split"].wait(eng, b)
        for c in range(KT):
            cols = slice(c * P, (c + 1) * P)
            mm = split_product(
                eng, ps[:, c * S:(c + 1) * S],
                [(core.hi["v"][:, kt, cols], core.lo["v"][:, kt, cols]) for kt in range(KT)],
                [(core.hi["p"][:, kt, :], core.lo["p"][:, kt, :]) for kt in range(KT)])
        core.e["p_o"].at(mm)
        core.e["e1"].wait(eng, b, 1)
        for qt in range(KT):
            for kt in range(KT):
                mm = eng.matmul(den[:, qt:qt + 1], core.prob[:, kt, qt * P:(qt + 1) * P], core.ones[:, 0:1],
                                start=kt == 0, stop=kt == KT - 1)
        core.e["p_den"].at(mm)
    elif name == "scalar":
        core.e["p_o"].wait(eng, b)
        core.e["p_v"].wait(eng, b, 0)
        core.e["oT_hi"].at(eng.activation(core.tr_hi[0][:, :, :], ps[:, :], ACT.Copy))
    elif name == "vector":
        core.e["oT_hi"].wait(eng, b)
        core.e["oT_lo"].at(eng.tensor_tensor(core.tr_lo[0][:, :, :], ps[:, :], core.tr_hi[0][:, :, :].bitcast(F32),
                                          ALU.subtract))
        core.e["p_den"].wait(eng, b)
        core.e["den"].at(eng.reciprocal(core.r_den[:, :], den[:, 0:KT]))


def st_self_output(core, name, eng, b, it):
    ps = core.psum[1]
    if name == "tensor":
        core.e["oT_lo"].wait(eng, b, 0)
        core.e["oT_lo"].wait(eng, b)
        w_hi, w_lo = core.w["attn", "Wo"]
        for t in range(KT):
            rows = slice(t * P, (t + 1) * P)
            mm = split_product(
                eng, ps[:, t * D:(t + 1) * D],
                [(core.tr_hi[0][:, c, rows], core.tr_lo[0][:, c, rows]) for c in range(KT)],
                [(w_hi[:, c, :], w_lo[:, c, :]) for c in range(KT)])
        core.e["p_y"].at(mm)
    elif name == "vector":
        core.e["p_y"].wait(eng, b)
        core.e["den"].wait(eng, b)
        core.e["xb"].wait(eng, b)
        core.e["resid1"].wait(eng, b.back(1))
        for t in range(KT):
            core.e["x1"].at(eng.scalar_tensor_tensor(core.x1[:, t, :], ps[:, t * D:(t + 1) * D],
                                                  core.r_den[:, t:t + 1], x2_of(core, b)[:, t, :],
                                                  ALU.mult, ALU.add))
    elif name == "gpsimd":
        core.e["x1"].wait(eng, b, apart=core.apart)
        bias = core.bias_row["xattn", "bo"][:, :].rearrange("p (o n) -> p o n", o=1).to_broadcast([P, KT, D])
        core.e["resid1"].at(eng.tensor_tensor(x2_of(core, b), core.x1[:, :, :], bias, ALU.add))


def st_cross_value(core, name, eng, b, it):
    ps = core.psum[1]
    if name == "tensor":
        core.e["x1"].wait(eng, b, 1)
        w_hi, w_lo = core.w["xattn", "Wv"]
        for t in range(KT):
            rows = slice(t * P, (t + 1) * P)
            mm = split_product(
                eng, ps[:, t * D:(t + 1) * D],
                [(core.tr_hi[1][:, c, rows], core.tr_lo[1][:, c, rows]) for c in range(KT)],
                [(w_hi[:, c, :], w_lo[:, c, :]) for c in range(KT)])
        core.e["p_cv"].at(mm)
    elif name == "vector":
        core.e["p_cv"].wait(eng, b)
        core.e["av"].wait(eng, b.back(2))
        for t in range(KT):
            core.e["cv"].at(eng.tensor_tensor(
                core.v_aug[b.p][:, t, :, 0:HD], ps[:, t * D:(t + 1) * D].rearrange("p (h d) -> p h d", h=H),
                core.bias_row["xattn", "bv"][:, :].rearrange("p (h d) -> p h d", h=H), ALU.add))


def st_scores(core, name, eng, b, it, i):
    base = 64 * b.p
    for qt in range(KT):
        ps, n = core.psum[3 + qt], 2 * i + qt
        if name == "tensor":
            if n == 0:
                core.q_stacked.wait(eng, b)
                core.k_stacked.wait(eng, b)
            if n >= 2:
                core.e["maxed"].wait(eng, b, n - 2)
            else:
                core.e["maxed"].wait(eng, b.back(1), 14 + n)
            eng.matmul(ps[:, :], core.ident_bf[:, :],
                       core.mask_q[:, qt:qt + 1, :].to_broadcast([P, 2, S]), start=True, stop=False,
                       skip_group_check=True)
            for h in range(2):
                mm = eng.matmul(ps[:, h * S:(h + 1) * S],
                                core.q_stack[base:base + 3 * HD, 2 * i + h, qt * P:(qt + 1) * P],
                                core.k_stack[base:base + 3 * HD, 2 * i + h, :], start=False, stop=True,
                                skip_group_check=True)
            core.e["s_tile"].at(mm)
        elif name == "vector":
            core.e["s_tile"].wait(eng, b, n)
            if n == 0:
                core.e["p_max"].wait(eng, b.back(1))
            core.e["maxed"].at(eng.tensor_reduce(core.neg_max[:, qt, 2 * i:2 * i + 2],
                                              ps[:, :].rearrange("p (h k) -> p h k", h=2), AX.X, ALU.max,
                                              negate=True))


def st_maxima(core, name, eng, b, it):
    ps = core.psum[0]
    if name == "tensor":
        if b.back(-1).inside(NB):
            core.e["den"].wait(eng, b.back(-1), 0)
        else:
            core.e["headsN"].wait(eng, b.back(1), 0)
        core.e["maxed"].wait(eng, b)
        for qt in range(KT):
            mm = eng.transpose(ps[0:H, qt * P:(qt + 1) * P], core.neg_max[:, qt, :], core.ident[:, :])
        core.e["p_max"].at(mm)
    elif name == "scalar":
        core.e["p_max"].wait(eng, b)
        core.m["stacked"].wait(eng, b.back(1))
        core.e["m_hi"].at(eng.activation(core.max_hi[0:H, :], ps[0:H, 0:S], ACT.Copy))
    elif name == "vector":
        core.e["m_hi"].wait(eng, b)
        core.e["m_lo"].at(eng.tensor_tensor(core.max_lo[0:H, :], ps[0:H, 0:S], core.max_hi[0:H, :].bitcast(F32),
                                         ALU.subtract))
    elif name == "sync":
        for r, part in enumerate((core.max_hi, core.max_lo)):
            if r == 0:
                core.e["m_hi"].wait(eng, b)
                core.e["s_tile"].wait(eng, b)
            else:
                core.e["m_lo"].wait(eng, b)
            row = 64 * b.p + 3 * HD + r
            core.m["stacked"].at(eng.dma_start(core.q_stack[row:row + 1, :, :].bitcast(F32),
                                            part[0:H, :].bitcast(F32)), b)


def st_exps(core, name, eng, b, it, i):
    base = 64 * b.p
    for kt in range(KT):
        ps, n = core.psum[5 + kt], 2 * i + kt
        if name == "tensor":
            if n == 0:
                core.m["stacked"].wait(eng, b)
            if n >= 2:
                core.e["exp"].wait(eng, b, n - 2)
            else:
                core.e["exp"].wait(eng, b.back(1), 14 + n)
            for h in range(2):
                eng.matmul(ps[:, h * S:(h + 1) * S],
                           core.k_stack[base:base + 3 * HD + 2, 2 * i + h, kt * P:(kt + 1) * P],
                           core.q_stack[base:base + 3 * HD + 2, 2 * i + h, :], start=h == 0, stop=False,
                           skip_group_check=True)
            mm = eng.matmul(ps[:, :], core.ident_bf[:, :],
                            core.mask_k[:, kt:kt + 1, :].to_broadcast([P, 2, S]), start=False, stop=True,
                            skip_group_check=True)
            core.e["t_tile"].at(mm)
        elif name == "scalar":
            core.e["t_tile"].wait(eng, b, n)
            if n % 4 == 0:
                g = n // 4
                if g >= 2:
                    core.e["av"].wait(eng, b, g - 2)
                else:
                    core.e["av"].wait(eng, b.back(1), g + 2)
            core.e["exp"].at(eng.activation(core.exp_ring[:, n % 8, :, :], ps[:, :], ACT.Exp, scale=HD ** -0.5))


def st_weighted(core, name, eng, b, it, g):
    ps = core.psum[7]
    if name == "tensor":
        if g == 0:
            core.e["cv"].wait(eng, b)
        if g == 2:
            core.e["av_out"].wait(eng, b, 0)
        if g == 0:
            core.e["av_out"].wait(eng, b.back(1), 1)
        core.e["exp"].wait(eng, b, 4 * g + 3)
        for kt in range(KT):
            for q in range(4):
                tile = 2 * (2 * g + q // 2) + kt
                mm = eng.matmul(ps[32 * q:32 * q + 32, (g % 2) * S:(g % 2 + 1) * S],
                                core.v_aug[b.p][:, kt, 4 * g + q, :], core.exp_ring[:, tile % 8, q % 2, :],
                                start=kt == 0, stop=kt == KT - 1, skip_group_check=True)
        core.e["av"].at(mm)
    elif name == "scalar" and g % 2 == 1:
        core.e["av"].wait(eng, b, g)
        if g == 1:
            core.e["p_headsT"].wait(eng, b.back(1))
        core.e["av_out"].at(eng.activation(core.heads_t[:, g - 1:g + 1, :], ps[:, :], ACT.Copy))


def st_heads_transposed(core, name, eng, b, it):
    for qt in range(KT):
        ps = core.psum[qt]
        if name == "tensor":
            if qt == 0:
                if b.back(-2).inside(NB):
                    core.e["q_square"].wait(eng, b.back(-2), 1)
                    core.e["q_split"].wait(eng, b.back(-2), 1)
                elif b.back(-1).inside(NB):
                    core.e["cq_split"].wait(eng, b.back(-1), 1)
                else:
                    core.e["xfT"].wait(eng, b.back(1), 0)
            elif qt == 1:
                if b.back(-2).inside(NB):
                    core.e["k_square"].wait(eng, b.back(-2), 1)
                    core.e["k_split"].wait(eng, b.back(-2), 1)
                elif b.back(-1).inside(NB):
                    core.e["xcT_lo"].wait(eng, b.back(-1), 0)
                else:
                    core.e["hT_lo"].wait(eng, b.back(1), 0)
            core.e["av_out"].wait(eng, b)
            for g in range(4):
                mm = eng.transpose(ps[:, g * P:(g + 1) * P], core.heads_t[:, g, qt * P:(qt + 1) * P],
                                   core.ident[:, :])
            core.e["p_headsT"].at(mm)
        elif name == "vector":
            core.e["p_headsT"].wait(eng, b, qt)
            view = ps[:, :].rearrange("p (h d) -> p h d", h=H)
            core.e["r_heads"].at(eng.reciprocal(core.r_heads[:, qt, :], view[:, :, HD]))
            core.e["r_heads"].wait(eng, b, qt)
            if qt == 0:
                core.e["p_hT"].wait(eng, b.back(1))
            scale = core.r_heads[:, qt, :].rearrange("p (h o) -> p h o", o=1).to_broadcast([P, H, HD])
            core.e["headsN"].at(eng.tensor_tensor(core.heads[:, qt, :].rearrange("p (h d) -> p h d", h=H),
                                               view[:, :, 0:HD], scale, ALU.mult))


def st_output(core, name, eng, b, it):
    ps = core.psum[2]
    if name == "tensor":
        if b.back(-2).inside(NB):
            core.e["ksq"].wait(eng, b.back(-2), 0)
        else:
            core.e["gate"].wait(eng, b.back(1), 0)
        core.e["hT_lo"].wait(eng, b)
        w_hi, w_lo = core.w["xattn", "Wo"]
        for t in range(KT):
            rows = slice(t * P, (t + 1) * P)
            mm = split_product(
                eng, ps[:, t * D:(t + 1) * D],
                [(core.tr_hi[1][:, c, rows], core.tr_lo[1][:, c, rows]) for c in range(KT)],
                [(w_hi[:, c, :], w_lo[:, c, :]) for c in range(KT)])
        core.e["p_y2"].at(mm)
    elif name == "vector":
        core.e["p_y2"].wait(eng, b)
        core.e["resid1"].wait(eng, b)
        core.e["x2"].at(eng.tensor_tensor(x2_of(core, b), ps[:, :].rearrange("p (t n) -> p t n", t=KT),
                                       x2_of(core, b), ALU.add))


def st_router_transpose(core, name, eng, b, it):
    ps = core.psum[0]
    if name == "tensor":
        if b.back(-1).inside(NB):
            core.e["m_lo"].wait(eng, b.back(-1), 0)
        else:
            core.e["headsN"].wait(eng, b, 0)
        core.e["ln2"].wait(eng, b)
        for c in range(KT):
            for t in range(KT):
                mm = eng.transpose(ps[:, c * S + t * P:c * S + (t + 1) * P],
                                   core.xn_ffn[:, t, c * P:(c + 1) * P], core.ident[:, :])
        core.e["p_xfT"].at(mm)
    elif name == "scalar":
        core.e["p_xfT"].wait(eng, b)
        core.e["p_gate"].wait(eng, b.back(1))
        core.e["xfT"].at(eng.activation(core.full[1][:, :, :], ps[:, :], ACT.Copy))


def st_router(core, name, eng, b, it):
    ps = core.psum[2]
    if name == "tensor":
        if b.back(-2).inside(NB):
            core.e["ck_split"].wait(eng, b.back(-2), 1)
        else:
            core.e["x2"].wait(eng, b, 0)
        core.e["xfT"].wait(eng, b)
        for t in range(KT):
            for c in range(KT):
                mm = eng.matmul(ps[:, t * NE:(t + 1) * NE], core.full[1][:, c, t * P:(t + 1) * P],
                                core.gate_w[:, c, :], start=c == 0, stop=c == KT - 1)
        core.e["p_gate"].at(mm)
    elif name == "vector":
        core.e["p_gate"].wait(eng, b)
        core.e["gate"].at(eng.tensor_copy(core.logits[:, bass.ds(b.v * KT, KT), :],
                                       ps[:, 0:KT * NE].rearrange("p (t n) -> p t n", t=KT)))


def attention_over(core, eng):
    last = Step(3, 1)
    core.e["gate"].wait(eng, last)
    core.e["xfT"].wait(eng, last)
    core.e["ln2_rstd"].wait(eng, last)
    core.e["resid1"].wait(eng, last)
    for b in (last.back(1), last):
        core.xn_stored.wait(eng, b)


def routing_sync(core, e):
    t, r = core.t, core.r
    e.dma_start(core.b1_rows[0:NE * FT, :], t["L0_ffn_b1"].rearrange("e (f p) -> (e f) p", p=P)).then_inc(r["b1_in"], 16)
    w1 = core.w1[:, :].rearrange("p (e k n) -> p e k n", e=NE, k=KT)
    w2 = core.w2[:, :].rearrange("p (e k n) -> p e k n", e=NE, k=FT)
    for x in range(NE):
        loads(core, e, w1[:, x], t["L0_ffn_W1"][x].rearrange("(k p) n -> p k n", p=P), core.E["experts_w1"])
        loads(core, e, w2[:, x], t["L0_ffn_W2"][x].rearrange("(k p) n -> p k n", p=P), core.E["experts_w2"])
    row = t["L0_ffn_b2"].rearrange("(a e) n -> a (e n)", a=1)
    loads(core, e, core.b2_row[:, :], row.partition_broadcast(P), core.E["experts_b"])


def routing_gpsimd(core, e):
    pool = core.r["pool"]
    e.iota(core.iota_i[:, :], pattern=[[1, P]], base=0, channel_multiplier=0).then_inc(pool, 1)
    e.iota(core.iota_p[:, :], pattern=[[P, TT]], base=1, channel_multiplier=1).then_inc(pool, 1)
    e.wait_ge(pool, 2)
    e.tensor_copy(core.iota_f[:, :], core.iota_i[:, :]).then_inc(pool, 1)
    e.tensor_copy(core.token_f[:, 0, :], core.iota_p[:, :]).then_inc(pool, 1)
    e.wait_ge(pool, 4)
    e.tensor_scalar(core.token_f[:, 1, :], core.token_f[:, 0, :], float(NB * S), None, ALU.add).then_inc(pool, 1)
    e.affine_select(out=core.strict[:, :], in_=core.ones[:, :], compare_op=ALU.is_gt, fill=0.0, base=0,
                    pattern=[[1, P]], channel_multiplier=-1).then_inc(pool, 1)


def routing_scalar(core, e):
    e.wait_ge(core.r["delta"], 1)
    e.activation(core.ex[:, :], core.delta[:, :], ACT.Exp).then_inc(core.r["ex"], 1)


def routing_tensor(core, e):
    r = core.r
    e.wait_ge(r["b1_in"], 16)
    n = NE * FT
    e.transpose(core.psum[3][:, 0:n], core.b1_rows[0:n, :], core.ident[0:n, 0:n]).then_inc(r["b1_t"], 1)
    e.wait_ge(r["pool"], 6)
    e.wait_ge(r["both"], 1)
    flat = core.both[:, :, :].rearrange("p t e -> p (t e)")
    e.matmul(core.psum[0][:, 0:TT * NE], core.strict[:, :], flat, start=True, stop=True)
    e.matmul(core.psum[1][:, 0:TT * NE], core.ones[:, :], flat, start=True, stop=True).then_inc(r["prefix"], 1)
    for n in range(2 * TT):
        e.wait_ge(r["slots"], n + 1)
        mm = e.matmul(core.psum[2][:, 0:2 * MAX_TILES], core.row_hot[n % 2][:, :],
                      core.tile_vals[n % 2][:, :, :].rearrange("p a t -> p (a t)"),
                      start=n == 0, stop=n == 2 * TT - 1)
        mm.then_inc(r["table"], 1)
    e.wait_ge(core.E["experts_w1"], 16 * NE)
    e.wait_ge(core.E["experts_w2"], 16 * NE)
    e.wait_ge(r["idx"], 1)


def routing_vector(core, e):
    r = core.r
    count = [0]

    def link(inst):
        inst.then_inc(r["vec"], 1)
        count[0] += 1
        return inst

    def settle():
        e.wait_ge(r["vec"], count[0])

    def bc(ap, shape, dim):
        return ap.unsqueeze(dim).to_broadcast(shape)

    for tt in range(TT):
        link(e.max(core.top8[:, tt, :], core.logits[:, tt, :]))
    settle()
    for tt in range(TT):
        link(e.max_index(core.idx8[:, tt, :], core.top8[:, tt, :], core.logits[:, tt, :]))
    e.tensor_tensor(core.delta[:, :], core.top8[:, :, 1], core.top8[:, :, 0], ALU.subtract)\
        .then_inc(r["delta"], 1)
    settle()
    link(e.tensor_copy(core.choice[:, :, :], core.idx8[:, :, 0:2]))
    settle()
    e.wait_ge(r["pool"], 6)
    for j in range(2):
        link(e.tensor_tensor(core.onehot[:, j, :, :], bc(core.iota_f[:, 0:NE], [P, TT, NE], 1),
                             bc(core.choice[:, :, j], [P, TT, NE], 2), ALU.is_equal))
    settle()
    e.tensor_tensor(core.both[:, :, :], core.onehot[:, 0, :, :], core.onehot[:, 1, :, :], ALU.add)\
        .then_inc(r["both"], 1)
    e.wait_ge(r["ex"], 1)
    link(e.tensor_scalar(core.one_plus[:, :], core.ex[:, :], 1.0, None, ALU.add))
    settle()
    link(e.reciprocal(core.weight[:, 0, :], core.one_plus[:, :]))
    settle()
    link(e.tensor_tensor(core.weight[:, 1, :], core.ex[:, :], core.weight[:, 0, :], ALU.mult))
    e.wait_ge(r["b1_t"], 1)
    e.tensor_copy(core.b1_cols[:, :], core.psum[3][:, 0:NE * FT]).then_inc(r["b1_cols"], 1)
    e.wait_ge(r["prefix"], 1)
    totals = core.psum[1][:, 0:TT * NE].rearrange("p (t e) -> p t e", e=NE)
    within = core.psum[0][:, 0:TT * NE].rearrange("p (t e) -> p t e", e=NE)
    link(e.tensor_copy(core.running[0][:, :, :], totals))
    settle()
    src, dst = core.running
    shift = 1
    while shift < TT:
        link(e.tensor_copy(dst[:, 0:shift, :], src[:, 0:shift, :]))
        link(e.tensor_tensor(dst[:, shift:, :], src[:, shift:, :], src[:, 0:TT - shift, :], ALU.add))
        settle()
        src, dst = dst, src
        shift *= 2
    link(e.scalar_tensor_tensor(out=core.cmp16[:, :, :], in0=bc(src[:, TT - 1, :], [P, NE, 16], 2),
                                scalar=1.0 / P, in1=bc(core.iota_f[:, 0:16], [P, NE, 16], 1),
                                op0=ALU.mult, op1=ALU.is_gt))
    link(e.tensor_tensor(core.slot_of[:, :, :], src[:, :, :], totals, ALU.subtract))
    settle()
    link(e.tensor_reduce(core.own_tiles[:, :], core.cmp16[:, :, :], AX.X, ALU.add))
    link(e.tensor_tensor(core.slot_of[:, :, :], core.slot_of[:, :, :], within, ALU.add))
    settle()
    src, dst = core.tiles_of
    link(e.tensor_copy(src[:, :], core.own_tiles[:, :]))
    settle()
    shift = 1
    while shift < NE:
        link(e.tensor_copy(dst[:, 0:shift], src[:, 0:shift]))
        link(e.tensor_tensor(dst[:, shift:], src[:, shift:], src[:, 0:NE - shift], ALU.add))
        settle()
        src, dst = dst, src
        shift *= 2
    n = MAX_TILES + 1
    link(e.tensor_tensor(core.cmp_tiles[:, :, :], bc(core.iota_f[:, 0:n], [P, n, NE - 1], 2),
                         bc(src[:, 0:NE - 1], [P, n, NE - 1], 1), ALU.is_ge))
    link(e.tensor_tensor(core.first_slot[:, :], src[:, :], core.own_tiles[:, :], ALU.subtract))
    settle()
    link(e.tensor_reduce(core.expert_f[:, :], core.cmp_tiles[:, :, :], AX.X, ALU.add))
    settle()
    link(e.tensor_copy(core.tile_expert[:, :], core.expert_f[:, :]))
    link(e.scalar_tensor_tensor(out=core.slot_of[:, :, :], in0=bc(core.first_slot[:, :], [P, TT, NE], 1),
                                scalar=float(P), in1=core.slot_of[:, :, :], op0=ALU.mult, op1=ALU.add))
    settle()
    for j in range(2):
        link(e.tensor_tensor(core.picked[:, :, :], core.slot_of[:, :, :], core.onehot[:, j, :, :], ALU.mult))
        settle()
        link(e.tensor_reduce(core.slot[:, j, :], core.picked[:, :, :], AX.X, ALU.add))
        settle()
    flat = core.slot[:, :, :].rearrange("p j t -> p (j t)")
    link(e.scalar_tensor_tensor(out=core.cmp_slots[:, :, :], in0=bc(flat, [P, 2 * TT, MAX_TILES], 2),
                                scalar=1.0 / P, in1=bc(core.iota_f[:, 1:1 + MAX_TILES], [P, 2 * TT, MAX_TILES], 1),
                                op0=ALU.mult, op1=ALU.is_ge))
    settle()
    tile_flat = core.slot_tile[:, :, :].rearrange("p j t -> p (j t)")
    link(e.tensor_reduce(tile_flat, core.cmp_slots[:, :, :], AX.X, ALU.add))
    settle()
    link(e.scalar_tensor_tensor(out=core.slot_row[:, :, :], in0=core.slot_tile[:, :, :], scalar=-float(P),
                                in1=core.slot[:, :, :], op0=ALU.mult, op1=ALU.add))
    settle()
    for n in range(2 * TT):
        j, tt = n // TT, n % TT
        if n >= 2:
            e.wait_ge(r["table"], n - 1)
        e.tensor_scalar(core.row_hot[n % 2][:, :], core.iota_f[:, :], core.slot_row[:, j, tt:tt + 1], None,
                        ALU.is_equal)
        for a, val in enumerate((core.token_f, core.weight)):
            ins = e.tensor_scalar(core.tile_vals[n % 2][:, a, :], core.iota_f[:, 0:MAX_TILES],
                                  core.slot_tile[:, j, tt:tt + 1], val[:, j, tt:tt + 1],
                                  ALU.is_equal, ALU.mult)
        ins.then_inc(r["slots"], 1)
    e.wait_ge(r["table"], 2 * TT)
    link(e.tensor_copy(core.slot_id[:, :], core.psum[2][:, 0:MAX_TILES]))
    link(e.tensor_copy(core.slot_weight[:, :], core.psum[2][:, MAX_TILES:2 * MAX_TILES]))
    settle()
    tmp = core.slot_tmp
    link(e.tensor_scalar(tmp[:, 0, :], core.slot_id[:, :], -1.0, 0.0, ALU.add, ALU.max))
    link(e.tensor_scalar(tmp[:, 1, :], core.slot_id[:, :], float(NB * S), float(NB * S), ALU.is_gt, ALU.mult))
    link(e.tensor_scalar(tmp[:, 2, :], core.slot_id[:, :], 0.0, 4.0 * NB * S, ALU.is_equal, ALU.mult))
    settle()
    link(e.tensor_tensor(core.gather_idx[:, :], tmp[:, 0, :], tmp[:, 1, :], ALU.subtract))
    link(e.scalar_tensor_tensor(out=core.scatter_idx[:, :], in0=core.slot_id[:, :], scalar=-1.0,
                                in1=tmp[:, 2, :], op0=ALU.add, op1=ALU.add))
    settle()
    e.tensor_copy(core.slot_tmp[:, 3, :], core.slot_id[:, :]).then_inc(r["idx"], 1)
    e.wait_ge(core.E["experts_b"], 16)


def experts(core, name, eng, it):
    def at(lag, fn):
        b = it.back(lag)
        if b.inside(MAX_TILES):
            fn(core, name, eng, b)

    if name == "gpsimd":
        if isinstance(it.v, int) and it.v == 0:
            eng.wait_ge(core.r["idx"], 1)
        at(0, ex_gather)
        at(4, ex_scatter)
        return
    at(3, ex_hidden_t)
    at(1, ex_rows_t)
    at(2, ex_hidden)
    at(3, ex_out)


def expert_of(core, eng, b):
    return eng.value_load(core.tile_expert[0:1, bass.ds(b.v, 1)], min_val=0, max_val=NE - 1)


def ex_gather(core, name, eng, b):
    core.rows_in.wait(eng, b.back(2), apart=core.apart)
    core.m["gnow"].at(eng.tensor_copy(core.gather_now[b.p][:, :], core.gather_idx[:, bass.ds(b.v, 1)]))
    core.m["gnow"].wait(eng, b, apart=core.apart)
    core.m["xT"].wait(eng, b.back(2), apart=core.apart)
    core.rows_in.at(eng.indirect_dma_start(
        core.slots_in[b.p][:, :], None, core.xn_dram,
        bass.IndirectOffsetOnAxis(ap=core.gather_now[b.p][:, :], axis=0)), b)


def ex_scatter(core, name, eng, b):
    core.rows_out.wait(eng, b.back(2), apart=core.apart)
    core.m["snow"].at(eng.tensor_copy(core.scatter_now[b.p][:, :], core.scatter_idx[:, bass.ds(b.v, 1)]))
    core.m["snow"].wait(eng, b, apart=core.apart)
    core.m["y"].wait(eng, b, apart=core.apart)
    core.rows_out.at(eng.indirect_dma_start(
        core.choice_dram, bass.IndirectOffsetOnAxis(ap=core.scatter_now[b.p][:, :], axis=0),
        core.y[b.p][:, :], None, bounds_check=2 * NB * S - 1, oob_is_err=False), b)


def ex_rows_t(core, name, eng, b):
    ps = core.psum[0]
    if name == "tensor":
        core.rows_in.wait(eng, b)
        core.m["slots_t"].wait(eng, b.back(1))
        for c in range(KT):
            mm = eng.transpose(ps[:, c * P:(c + 1) * P], core.slots_in[b.p][:, c * P:(c + 1) * P],
                               core.ident[:, :])
        core.m["xT"].at(mm)
    elif name == "scalar":
        core.m["xT"].wait(eng, b)
        core.m["hid"].wait(eng, b.back(2))
        core.m["slots_t"].at(eng.activation(core.slots_t[b.p][:, :, :], ps[:, 0:KT * P], ACT.Copy))


def ex_hidden(core, name, eng, b):
    if name == "tensor":
        x = expert_of(core, eng, b)
        core.m["slots_t"].wait(eng, b)
        for half in range(2):
            (core.m["hid_a"], core.m["hid_v"])[half].wait(eng, b.back(1))
            for c in range(KT):
                mm = eng.matmul(core.psum[1 + half][:, :], core.slots_t[b.p][:, c, :],
                                core.w1[:, bass.ds(x * (KT * FF) + (c * FF + half * 512), 512)],
                                start=c == 0, stop=c == KT - 1)
            core.m["hid"].at(mm)
    elif name == "scalar":
        core.m["hid"].wait(eng, b, 0)
        core.m["hidT"].wait(eng, b.back(2))
        core.m["hid_a"].at(eng.activation(core.hid[b.p][:, 0:512], core.psum[1][:, :], ACT.Copy))
    elif name == "vector":
        core.m["hid"].wait(eng, b, 1)
        core.m["hidT"].wait(eng, b.back(2))
        core.m["hid_v"].at(eng.tensor_copy(core.hid[b.p][:, 512:1024], core.psum[2][:, :]))


def ex_hidden_t(core, name, eng, b):
    half_tiles = FT // 2
    if name == "tensor":
        core.m["hid_a"].wait(eng, b)
        core.m["hid_v"].wait(eng, b)
        for half in range(2):
            (core.m["act_a"], core.m["act_v"])[half].wait(eng, b.back(1))
            for f in range(half_tiles):
                g = half * half_tiles + f
                mm = eng.transpose(core.psum[3 + half][:, f * P:(f + 1) * P],
                                   core.hid[b.p][:, g * P:(g + 1) * P], core.ident[:, :])
            core.m["hidT"].at(mm)
    elif name == "vector":
        x = expert_of(core, eng, b)
        core.m["act_a"].wait(eng, b.back(2))
        core.m["b1t"].at(eng.tensor_copy(core.b1_tile[b.p][:, :], core.b1_cols[:, bass.ds(x * FT, FT)]))
        core.m["b1t"].wait(eng, b)
        core.m["hidT"].wait(eng, b, 1)
        core.m["out"].wait(eng, b.back(2))
        for f in range(half_tiles):
            g = half_tiles + f
            core.m["act_v"].at(eng.tensor_scalar(core.hid_t[b.p][:, g, :], core.psum[4][:, f * P:(f + 1) * P],
                                              core.b1_tile[b.p][:, g:g + 1], 0.0, ALU.add, ALU.max))
    elif name == "scalar":
        core.m["b1t"].wait(eng, b)
        core.m["hidT"].wait(eng, b, 0)
        core.m["out"].wait(eng, b.back(2))
        for f in range(half_tiles):
            core.m["act_a"].at(eng.activation(core.hid_t[b.p][:, f, :], core.psum[3][:, f * P:(f + 1) * P],
                                           ACT.Relu, bias=core.b1_tile[b.p][:, f:f + 1]))


def ex_out(core, name, eng, b):
    ps = core.psum[5 + b.p]
    if name == "tensor":
        x = expert_of(core, eng, b)
        core.m["act_a"].wait(eng, b)
        core.m["act_v"].wait(eng, b)
        core.m["y"].wait(eng, b.back(2), 0)
        for f in range(FT):
            mm = eng.matmul(ps[:, 0:D], core.hid_t[b.p][:, f, :],
                            core.w2[:, bass.ds(x * (FT * D) + f * D, D)], start=f == 0, stop=f == FT - 1)
        core.m["out"].at(mm)
    elif name == "vector":
        x = expert_of(core, eng, b)
        core.m["out"].wait(eng, b)
        core.rows_out.wait(eng, b.back(2))
        core.m["y"].at(eng.tensor_tensor(core.y[b.p][:, :], ps[:, 0:D], core.b2_row[:, bass.ds(x * D, D)], ALU.add))
        core.m["y"].wait(eng, b, 0)
        core.m["y"].at(eng.tensor_scalar(core.y[b.p][:, :], core.y[b.p][:, :],
                                      core.slot_weight[:, bass.ds(b.v, 1)], None, ALU.mult))


def finish_gpsimd(core, e):
    pass


def finish_scalar(core, e):
    pass


def finish_tensor(core, e):
    pass


def finish_sync(core, e):
    for i in (MAX_TILES - 2, MAX_TILES - 1):
        core.rows_out.wait(e, Step(i // 2, i % 2))
    core.m["out"].wait(e, Step((MAX_TILES - 1) // 2, (MAX_TILES - 1) % 2))
    rows = core.choice_dram.rearrange("(j t p) d -> p j t d", j=2, p=P)
    out = core.out.rearrange("b (t p) d -> p (b t) d", p=P)
    for c in range(TT // 4):
        step = Step(c // 2, c % 2)
        if c >= 2:
            e.wait_ge(core.sums, 2 * (c - 1))
            e.dma_start(out[:, 4 * (c - 2):4 * (c - 1), :], core.x2[:, 4 * (c - 2):4 * (c - 1), :]).then_inc(core.stored, 16)
        for j in range(2):
            core.choice_in.at(e.dma_start(core.choice_rows[c % 2][:, j, :, :], rows[:, j, 4 * c:4 * c + 4, :]), step)
    for c in range(TT // 4 - 2, TT // 4):
        e.wait_ge(core.sums, 2 * (c + 1))
        e.dma_start(out[:, 4 * c:4 * c + 4, :], core.x2[:, 4 * c:4 * c + 4, :]).then_inc(core.stored, 16)
    e.wait_ge(core.stored, 16 * (TT // 4))


def finish_vector(core, e):
    for c in range(TT // 4):
        for j in range(2):
            if j == 0:
                e.wait_ge(core.choice_in.sems[c % 2], 32 * (c // 2 + 1))
            else:
                e.wait_ge(core.sums, 2 * c + 1)
            rows = core.x2[:, 4 * c:4 * c + 4, :]
            e.tensor_tensor(rows, rows, core.choice_rows[c % 2][:, j, :, :], ALU.add).then_inc(core.sums, 1)


INPUTS = ["x", "ctx_1024", "mask_1x1xSxS2_ik0"] + [
    f"L0_{m}_{n}" for m in ("attn", "xattn") for n in ("Wq", "bq", "Wk", "bk", "Wv", "bv", "Wo", "bo")] + [
    f"L0_ffn_{n}" for n in ("Wg", "W1", "b1", "W2", "b2")]


def kernel(**inputs):
    import numpy as np
    import concourse.bacc as bacc
    from concourse.bass_utils import run_bass_kernel_spmd

    nc = bacc.Bacc("TRN2", target_bir_lowering=False, num_devices=1)
    arrays = {n: np.ascontiguousarray(inputs[n]) for n in INPUTS}
    handles = {n: nc.dram_tensor(n, a.shape, mybir.dt.from_np(a.dtype), kind="ExternalInput").ap()
               for n, a in arrays.items()}
    out = nc.dram_tensor("out", (NB, S, D), F32, kind="ExternalOutput").ap()
    build(nc, handles, out)
    result = run_bass_kernel_spmd(nc, [arrays], core_ids=[0])
    return result.results[0]["out"]
```

```python
from contextlib import ExitStack
from functools import partial

import concourse.bass as bass
from concourse import mybir

F32 = mybir.dt.float32
F32R = mybir.dt.float32r
BF16 = mybir.dt.bfloat16
I32 = mybir.dt.int32
U32 = mybir.dt.uint32
ALU = mybir.AluOpType
ACT = mybir.ActivationFunctionType
AX = mybir.AxisListType

P = 128
NB = 8
S = 256
D = 256
KT = D // P
H = 16
HD = D // H
NE = 8
FF = 1024
FT = FF // P
TT = NB * S // P
EPS = 1e-5
MASKED = -(2.0 ** 120)
WEIGHTS = [(m, n) for m in ("attn", "xattn") for n in ("Wq", "Wk", "Wv", "Wo")]
ATT_LAG = 2
MOE_LAG = 4
PLACE = KT * FF + FT * D
CHUNK = 2
CHUNKS = NB * S // P // CHUNK
EARLY = 2
MAX_TILES = (2 * NB * S + NE * (P - 1)) // P
COLS = (MAX_TILES + 1) // 2 * 2


class Step:

    def __init__(self, j, u):
        self.j, self.u = j, u
        self.v = 2 * j + u
        self.p = u

    def back(self, k):
        n = self.u - k
        return Step(self.j + n // 2, n % 2)

    def inside(self, count):
        return not isinstance(self.v, int) or 0 <= self.v < count


def pipeline(eng, count, lag, body, first=2, ahead=0):
    for n in range(-ahead, first):
        body(Step(n // 2, n % 2))
    pairs = (count - first - ahead) // 2
    with eng.Fori(first // 2, first // 2 + pairs) as j:
        for u in range(2):
            body(Step(j, u))
    for n in range(first + 2 * pairs, count + lag):
        body(Step(n // 2, n % 2))


def wait_count(eng, sem, count, apart):
    if apart is not None and not isinstance(count, int):
        register, passed = apart
        eng.reg_mov(register, count)
        count = eng.snap(register)
        eng.wait_ge(passed, 16)
    eng.wait_ge(sem, count)


class Event:

    def __init__(self, sem, per=1, unit=1):
        self.sem, self.per, self.unit = sem, per, unit

    def at(self, inst):
        inst.then_inc(self.sem, self.unit)

    def wait(self, eng, step, k=None, apart=None):
        if isinstance(step.v, int) and step.v < 0:
            return
        n = self.per if k is None else k + 1
        wait_count(eng, self.sem, step.j * (2 * self.per * self.unit) + (step.u * self.per + n) * self.unit, apart)


class ParityDma:

    def __init__(self, sems, per=1):
        self.sems, self.per = sems, per

    def at(self, inst, step):
        inst.then_inc(self.sems[step.p], 16)

    def wait(self, eng, step, apart=None):
        if isinstance(step.v, int) and step.v < 0:
            return
        wait_count(eng, self.sems[step.p], step.j * (16 * self.per) + 16 * self.per, apart)


def build(nc, inputs, out):
    with ExitStack() as ctx:
        run(Core(nc, inputs, out, ctx))


class Core:

    def __init__(self, nc, t, out, ctx):
        self.nc, self.t, self.out, self.ctx = nc, t, out, ctx
        self.e, self.m, self.hi, self.lo = {}, {}, {}, {}
        self.xn_dram = nc.dram_tensor("xn_rows", (NB * S, D), F32).ap()
        self.choice_dram = nc.dram_tensor("choice_rows_dram", (2 * NB * S, D), F32).ap()


def sem(core, name):
    return core.ctx.enter_context(core.nc.semaphore(name))


def event(core, name, per=1):
    return Event(sem(core, name), per)


def dma_event(core, name, per=1):
    return ParityDma([sem(core, f"{name}{i}") for i in range(2)], per)


def run(core):
    nc, t = core.nc, core.t
    core.psum = [core.ctx.enter_context(nc.psum_tensor(f"bank{i}", [P, 512], F32)) for i in range(8)]
    top = nc.sbuf_usable_end
    core.base = (nc.sbuf_base + 63) // 64 * 64
    core.cursor = core.base
    core.top = top
    plan_shared(core)
    shared_end = core.cursor
    plan_attention(core)
    core.attention_end = core.cursor
    core.cursor = shared_end
    plan_experts(core)
    make_events(core)
    block = core.ctx.enter_context(nc.Block())
    programs = {
        "sync": (block.sync, setup_sync, routing_sync, finish_sync),
        "gpsimd": (block.gpsimd, setup_gpsimd, routing_gpsimd, finish_gpsimd),
        "scalar": (block.scalar, setup_scalar, routing_scalar, finish_scalar),
        "tensor": (block.tensor, setup_tensor, routing_tensor, finish_tensor),
        "vector": (block.vector, setup_vector, routing_vector, finish_vector),
    }
    for name, (engine, setup, routing, finish) in programs.items():
        @engine
        def _(eng, name=name, setup=setup, routing=routing, finish=finish):
            core.apart = (eng.alloc_register(f"{name}_count"), core.E["x_first0"])
            setup(core, eng)
            pipeline(eng, NB, ATT_LAG, lambda it: attention(core, name, eng, it), ahead=1)
            attention_over(core, eng)
            routing(core, eng)
            pipeline(eng, MAX_TILES, MOE_LAG, lambda it: experts(core, name, eng, it), first=6)
            finish(core, eng)


def buffer(core, name, free, dt=F32, parts=P):
    size = {F32: 4, F32R: 4, BF16: 2, I32: 4, U32: 4}[dt]
    n = 1
    for f in free:
        n *= f
    handle = core.nc.alloc_sbuf_tensor_at(name, [parts, *free], dt, offset=core.cursor, align_bytes=32)
    core.cursor += (n * size + 31) // 32 * 32
    assert core.cursor <= core.top, (name, core.cursor, core.top)
    return handle


def plan_shared(core):
    core.ident = buffer(core, "ident", [P])
    core.ones = buffer(core, "ones", [P])
    core.x2 = buffer(core, "x2", [TT, D])
    core.logits = buffer(core, "logits", [TT, NE])
    core.gate_w = buffer(core, "gate_w", [KT, NE])
    core.top8 = buffer(core, "top8", [TT, 8])
    core.idx8 = buffer(core, "idx8", [TT, 8], U32)
    core.tile_expert = buffer(core, "tile_expert", [MAX_TILES + 1], I32)
    core.tile_loads = buffer(core, "tile_loads", [MAX_TILES + 1], I32)
    core.gather_idx = buffer(core, "gather_idx", [MAX_TILES], U32)
    core.scatter_idx = buffer(core, "scatter_idx", [MAX_TILES], U32)
    core.slot_weight = buffer(core, "slot_weight", [MAX_TILES])


def plan_attention(core):
    sb = partial(buffer, core)
    core.ident_bf = sb("ident_bf", [P], BF16)
    core.neg_half = sb("neg_half", [P])
    core.ctx_in = sb("ctx_in", [KT, D])
    core.xn = sb("xn", [KT, D])
    core.xn_cross = sb("xn_cross", [KT, D])
    core.xn_ffn = sb("xn_ffn", [KT, D])
    core.x1 = sb("x1", [KT, D])
    core.tr_hi = [sb(f"tr_hi{i}", [KT, S], F32R) for i in range(2)]
    core.tr_lo = [sb(f"tr_lo{i}", [KT, S], F32R) for i in range(2)]
    core.full = [sb(f"full{i}", [KT, S]) for i in range(2)]
    for n in ("q", "k", "v", "cq", "ck", "p"):
        core.hi[n] = sb(n + "_hi", [KT, S], F32R)
        core.lo[n] = sb(n + "_lo", [KT, S], F32R)
    core.q_sq, core.k_sq = sb("q_sq", [KT, S]), sb("k_sq", [KT, S])
    core.prob = sb("prob", [KT, S])
    core.q_stack = sb("q_stack", [H, S], F32R)
    core.k_stack = sb("k_stack", [H, S], F32R)
    core.v_aug = [sb(f"v_aug{i}", [KT, H, 32]) for i in range(2)]
    core.exp_ring = sb("exp_ring", [8, 2, S])
    core.heads_t = sb("heads_t", [4, S])
    core.heads = sb("heads", [KT, D])
    core.w = {}
    for n in ("Wq", "Wk", "Wv", "Wo"):
        for m in ("attn", "xattn"):
            core.w[m, n] = (sb(f"{m}{n}h", [KT, D], F32R), sb(f"{m}{n}l", [KT, D], F32R))
    core.bias_row = {k: sb("bias_" + "_".join(k), [D])
                     for k in (("attn", "bv"), ("attn", "bo"), ("xattn", "bv"), ("xattn", "bo"))}
    core.bias_col = {k: sb("bias_" + "_".join(k), [KT])
                     for k in (("attn", "bq"), ("attn", "bk"), ("xattn", "bq"), ("xattn", "bk"))}
    core.mask_q = sb("mask_q", [KT, S], BF16)
    core.mask_k = sb("mask_k", [KT, S], BF16)
    core.stats = sb("stats", [3, KT, 6])
    core.moments = sb("moments", [3, KT, 2])
    core.rstd = sb("rstd", [3, KT])
    core.minus_half = sb("minus_half", [KT])
    core.neg_ksq = sb("neg_ksq", [KT])
    core.r_den = sb("r_den", [KT])
    core.neg_max = sb("neg_max", [KT, H])
    core.max_hi = sb("max_hi", [S], F32R)
    core.max_lo = sb("max_lo", [S], F32R)
    core.r_heads = sb("r_heads", [KT, H])
    core.one_rows = sb("one_rows", [S], F32R, parts=1)
    core.mask_int = core.full[0][:, :, :].bitcast(I32)


def plan_experts(core):
    sb = partial(buffer, core)
    core.b1_rows = sb("b1_rows", [P])
    core.b1_cols = sb("b1_cols", [NE * FT])
    core.b2_row = sb("b2_row", [NE * D])
    core.slots_in = [sb(f"slots_in{i}", [D]) for i in range(2)]
    core.slots_t = [sb(f"slots_t{i}", [KT, P]) for i in range(2)]
    core.hid_t = [sb(f"hid_t{i}", [FT, P]) for i in range(2)]
    core.y = [sb(f"y{i}", [D]) for i in range(2)]
    core.b1_tile = [sb(f"b1_tile{i}", [FT]) for i in range(2)]
    after = core.cursor
    core.gather_now = [sb(f"gather_now{i}", [1], U32) for i in range(2)]
    core.scatter_now = [sb(f"scatter_now{i}", [1], U32) for i in range(2)]
    core.choice = sb("choice", [TT, 2])
    core.onehot = sb("onehot", [2, TT, NE])
    core.both = sb("both", [TT, NE])
    core.running = [sb(f"running{i}", [TT, NE]) for i in range(2)]
    core.slot_of = sb("slot_of", [TT, NE])
    core.picked = sb("picked", [TT, NE])
    core.slot = sb("slot", [2, TT])
    core.cmp16 = sb("cmp16", [NE, 16])
    core.tiles_of = [sb(f"tiles_of{i}", [NE]) for i in range(2)]
    core.first_slot = sb("first_slot", [NE])
    core.cmp_tiles = sb("cmp_tiles", [MAX_TILES + 1, NE - 1])
    core.expert_f = sb("expert_f", [MAX_TILES + 1])
    core.loads_f = sb("loads_f", [MAX_TILES + 1])
    core.iota_i = sb("iota_i", [P], I32)
    core.iota_f = sb("iota_f", [P])
    core.iota_p = sb("iota_p", [TT], I32)
    core.token_f = sb("token_f", [2, TT])
    core.strict = sb("strict", [P])
    core.delta = sb("delta", [TT])
    core.ex = sb("ex", [TT])
    core.one_plus = sb("one_plus", [TT])
    core.weight = sb("weight", [2, TT])
    core.slot_tile = sb("slot_tile", [2, TT])
    core.slot_row = sb("slot_row", [2, TT])
    core.own_tiles = sb("own_tiles", [NE])
    core.slot_int, core.tile_int, core.row_int = (sb(n, [2, TT], I32) for n in ("slot_int", "tile_int", "row_int"))
    core.weight_hi, core.weight_lo = sb("weight_hi", [2, TT], F32R), sb("weight_lo", [2, TT])
    tables = core.cursor
    core.row_hot = [sb(f"row_hot{j}", [TT // 2, P], F32R) for j in range(2)]
    core.tile_hot = sb("tile_hot", [TT // 2, COLS])
    core.tile_vals = [sb(f"tile_vals{j}", [TT // 2, 3, COLS], F32R) for j in range(2)]
    tables_end = core.cursor
    core.cursor = tables
    core.w1_now = [sb(f"w1_now{i}", [KT * FF]) for i in range(2)]
    core.cursor = max(core.cursor, tables_end)
    core.slot_id = sb("slot_id", [MAX_TILES])
    core.slot_tmp = sb("slot_tmp", [4, MAX_TILES])
    places = core.top // 32 * 32 - NE * PLACE * 4
    assert places >= core.cursor and places + (NE - EARLY) * PLACE * 4 >= core.attention_end
    core.cursor = places
    core.experts_w = sb("experts_w", [NE * PLACE])
    core.cursor = places
    core.choice_rows = [sb(f"choice_rows{i}", [2, CHUNK, D]) for i in range(CHUNKS)]


def make_events(core):
    ev = partial(event, core)
    dma = partial(dma_event, core)
    E = core.E = {}
    for n in "x_first0 x_first1 x_rest consts_in weights weights_rest mask_in experts_in experts_b".split():
        E[n] = sem(core, n)
    for n in "const_pool const_vec weights_split masks_ready neg_mask prior_pool".split():
        E[n] = sem(core, n)
    core.ctx_loaded = dma("ctx_loaded")
    core.q_stacked, core.k_stacked = dma("q_stacked", 6), dma("k_stacked", 6)
    core.m["stacked"] = dma("m_stacked", 2)
    core.xn_stored = dma("xn_stored")
    per = dict(
        ln0_stats=4, ln0_eps=1, ln0_rstd=1, ln0=2, ln1_stats=4, ln1_eps=1, ln1_rstd=1, ln1=2,
        ln2_stats=4, ln2_eps=1, ln2_rstd=1, ln2=2,
        xb=1, resid1=1,
        p_xnT=1, p_q=1, p_k=1, p_v=1, p_ksq=1, p_s1=1, p_o=1, p_den=1, p_y=1, p_xcT=1, p_cq=1,
        p_ctxT=1, p_ck=1, p_cv=1, p_max=1, p_headsT=2, p_hT=1, p_y2=1, p_xfT=1, p_gate=1,
        s_tile=16, t_tile=16, av=4,
        xnT_hi=1, xnT_lo=1, q_hi=2, k_hi=2, v_full=1, q_square=2, q_norm=1, k_square=2,
        q_split=2, k_split=2, v_hi=1, v_split=1, ksq=1, e1=2, e2=1, p_hi=1, p_split=1, oT_hi=1, oT_lo=1, den=1, x1=2,
        xcT_hi=1, xcT_lo=1, cq_hi=2, cq_split=2, ctxT_hi=1, ctxT_lo=1, ck_hi=2, ck_split=2,
        cv=2, maxed=16, m_hi=1, m_lo=1, exp=16, av_out=2, r_heads=2, headsN=2, hT_hi=1, hT_lo=1,
        x2=1, xfT=1, gate=1,
    )
    for n, k in per.items():
        core.e[n] = ev("e_" + n, k)
    core.r = {n: sem(core, "r_" + n) for n in
              "best vec pool act both prefix delta ex slots table idx b1_in b1_t b1_cols".split()}
    core.rows_in, core.rows_out = dma_event(core, "rows_in"), dma_event(core, "rows_out")
    per = dict(gnow=1, snow=1, xT=1, slots_t=1, w1=1, hid=2, act_a=4, act_v=4, b1t=1,
               out=1, y=2)
    for n, k in per.items():
        core.m[n] = ev("m_" + n, k)
    core.sums, core.stored = sem(core, "sums"), sem(core, "stored")
    core.choice_in = [sem(core, f"choice_in{c}") for c in range(CHUNKS)]


def loads(core, eng, dst, src, sem):
    eng.dma_start(dst, src).then_inc(sem, 16)


def x2_of(core, b):
    return core.x2[:, bass.ds(b.v * KT, KT), :]


def setup_sync(core, e):
    t, E = core.t, core.E
    x_rows = t["x"].rearrange("b (t p) d -> p (b t) d", p=P)
    for b in range(2):
        loads(core, e, core.x2[:, b * KT:(b + 1) * KT, :], x_rows[:, b * KT:(b + 1) * KT, :], E[f"x_first{b}"])
    for i, (m, n) in enumerate(WEIGHTS):
        loads(core, e, raw_weight(core, i), t[f"L0_{m}_{n}"].rearrange("(k p) n -> p k n", p=P),
                   E["weights" if i < 3 else "weights_rest"])


def raw_weight(core, i):
    return core.exp_ring[:, i, :, :]


def weight_pieces(core):
    pieces = []
    for i, key in enumerate(WEIGHTS):
        raw, (hi, lo) = raw_weight(core, i), core.w[key]
        if key in (("xattn", "Wq"), ("xattn", "Wk")):
            for k in range(KT):
                pieces.append((raw[:, k, :].rearrange("p (c h d) -> p c d h", c=KT, d=HD),
                               *(w[:, k, :].rearrange("p (c d h) -> p c d h", c=KT, d=HD) for w in (hi, lo))))
        else:
            pieces.append((raw, hi[:, :, :], lo[:, :, :]))
    return pieces


def setup_scalar(core, e):
    t, E = core.t, core.E
    mask = t["mask_1x1xSxS2_ik0"].rearrange("a b q k -> (a b q) k")
    loads(core, e, core.mask_int, mask.rearrange("(t p) k -> p t k", p=P), E["mask_in"])
    for (m, n), dst in core.bias_col.items():
        with core.nc.allow_non_contiguous_dma("256 bias values, one per partition"):
            for k in range(KT):
                col = t[f"L0_{m}_{n}"][k * P:(k + 1) * P]
                col = (col.rearrange("(h d o) -> d h o", d=HD, o=1) if m == "xattn"
                       else col.rearrange("(p o) -> p o", o=1))
                loads(core, e, dst[:, k:k + 1], col, E["consts_in"])
    for (m, n), dst in core.bias_row.items():
        row = t[f"L0_{m}_{n}"].rearrange("(a n) -> a n", a=1)
        loads(core, e, dst[:, :], row.partition_broadcast(P), E["consts_in"])
    loads(core, e, core.gate_w[:, :, :], t["L0_ffn_Wg"].rearrange("(k p) n -> p k n", p=P), E["consts_in"])
    e.wait_ge(E["neg_mask"], 2)
    e.activation(core.mask_k[:, :, :], core.psum[7][:, :], ACT.Copy).then_inc(E["masks_ready"], 1)


def setup_gpsimd(core, e):
    E, pool = core.E, core.E["const_pool"]
    e.memset(core.ident[:, :], 0.0).then_inc(pool, 1)
    e.wait_ge(pool, 1)
    e.affine_select(out=core.ident[:, :], in_=core.ident[:, :], compare_op=ALU.not_equal, fill=1.0,
                    base=0, pattern=[[-1, P]], channel_multiplier=1).then_inc(pool, 1)
    e.memset(core.ones[:, :], 1.0).then_inc(pool, 1)
    e.memset(core.neg_half[:, :], -0.5).then_inc(pool, 1)
    e.memset(core.minus_half[:, :], -0.5).then_inc(pool, 1)
    e.wait_ge(pool, 2)
    e.tensor_copy(core.ident_bf[:, :], core.ident[:, :]).then_inc(pool, 1)
    for i in range(2):
        e.memset(core.v_aug[i][:, :, :, :], 0.0).then_inc(pool, 1)
    e.wait_ge(pool, 8)
    for i in range(2):
        e.memset(core.v_aug[i][:, :, :, HD:HD + 1], 1.0).then_inc(pool, 1)
    e.wait_ge(pool, 3)
    e.tensor_copy(core.one_rows[:, :], core.ones[0:1, 0:1].to_broadcast([1, S])).then_inc(pool, 1)
    e.wait_ge(pool, 11)
    for p in range(2):
        for r in range(2):
            row = 64 * p + 3 * HD + r
            e.dma_start(core.k_stack[row:row + 1, :, :].bitcast(F32),
                        core.one_rows[0:1, :].bitcast(F32).rearrange("a (o s) -> a o s", o=1).to_broadcast([1, H, S])
                        ).then_inc(E["prior_pool"], 16)


def setup_vector(core, e):
    E = core.E
    e.wait_ge(E["mask_in"], 16)
    e.tensor_scalar(core.mask_q[:, :, :], core.mask_int, 0.0, MASKED, ALU.is_equal, ALU.mult)\
        .then_inc(E["neg_mask"], 1)


def setup_tensor(core, e):
    E = core.E
    e.wait_ge(E["const_pool"], 11)
    e.wait_ge(E["neg_mask"], 1)
    for kt in range(KT):
        for qt in range(KT):
            mm = e.matmul(core.psum[7][:, kt * S + qt * P:kt * S + (qt + 1) * P],
                          core.mask_q[:, qt, kt * P:(kt + 1) * P], core.ident_bf[:, :], start=True, stop=True)
    mm.then_inc(E["neg_mask"], 1)


def split_weights(core, name, e, first, count, loads_sem, loads_count):
    E, pieces = core.E, weight_pieces(core)
    if name == "scalar":
        e.wait_ge(E[loads_sem], loads_count)
    for i in range(first, first + count):
        raw, hi, lo = pieces[i]
        if name == "scalar":
            e.activation(hi, raw, ACT.Copy).then_inc(E["weights_split"], 1)
        elif name == "vector":
            e.wait_ge(E["weights_split"], i + 1)
            e.tensor_tensor(lo, raw, hi.bitcast(F32), ALU.subtract).then_inc(E["const_vec"], 1)
    if name == "tensor" and first == 0:
        e.wait_ge(E["const_vec"], count)
        e.wait_ge(E["prior_pool"], 64)
        e.wait_ge(E["masks_ready"], 1)
        e.wait_ge(E["consts_in"], 16 * 13)


def attention(core, name, eng, it):
    def at(lag, fn, *args):
        b = it.back(lag)
        if b.inside(NB):
            fn(core, name, eng, b, it, *args)

    if name == "sync" and isinstance(it.v, int) and it.v == 1:
        for x in range(EARLY):
            load_expert(core, eng, x, core.E["experts_in"])
    starting = isinstance(it.v, int) and it.v == 0
    if starting:
        split_weights(core, name, eng, 0, 3, "weights", 16 * 3)
    at(1, st_scores, 0)
    at(0, st_project, "q")
    at(1, st_scores, 1)
    at(0, st_project, "k")
    if starting:
        split_weights(core, name, eng, 3, len(weight_pieces(core)) - 3, "weights_rest", 16 * 5)
    if starting and name == "sync":
        core.e["p_q"].wait(eng, it)
        rows = core.t["x"].rearrange("b (t p) d -> p (b t) d", p=P)
        loads(core, eng, core.x2[:, 2 * KT:, :], rows[:, 2 * KT:, :], core.E["x_rest"])
    at(1, st_scores, 2)
    at(2, st_heads_transposed)
    at(0, st_value)
    at(1, st_scores, 3)
    at(0, st_key_norms)
    at(2, st_transpose, "hT")
    at(0, st_rbf)
    at(1, st_scores, 4)
    at(2, st_output)
    at(0, st_rbf_split)
    at(1, st_scores, 5)
    at(0, st_transpose, "ctxT")
    at(0, st_rbf_out)
    at(1, st_scores, 6)
    at(2, st_moments, 2)
    at(1, st_scores, 7)
    if starting and name == "tensor":
        eng.wait_ge(core.E["const_vec"], len(weight_pieces(core)))
    if name != "gpsimd":
        at(0, st_self_output)
    at(0, st_moments, 1)
    if name == "gpsimd":
        at(0, st_self_output)
    at(2, st_normalise, 2)
    at(1, st_maxima)
    at(0, st_normalise, 1)
    at(0, st_project, "ck")
    at(0, st_cross_value)
    at(2, st_router_transpose)
    at(0, st_transpose, "xcT")
    at(2, st_router)
    at(1, st_exps, 0)
    at(0, st_project, "cq")
    at(1, st_exps, 1)
    at(1, st_exps, 2)
    at(1, st_weighted, 0)
    at(1, st_exps, 3)
    if name == "vector" and isinstance(it.v, int) and it.v == NB:
        core.e["gate"].wait(eng, it.back(2))
        best_experts(core, eng, 0, TT - KT)
    at(-1, st_moments, 0)
    at(1, st_exps, 4)
    at(1, st_weighted, 1)
    at(-1, st_normalise, 0)
    at(1, st_exps, 5)
    at(1, st_exps, 6)
    at(1, st_weighted, 2)
    at(1, st_exps, 7)
    at(-1, st_transpose, "xnT")
    at(1, st_weighted, 3)

def st_moments(core, name, eng, b, it, n):
    stats, eps_done, rstd_done, done = (core.e[f"ln{n}{x}"] for x in ("_stats", "_eps", "_rstd", ""))
    if name == "vector":
        src = core.x1[:, :, :] if n == 1 else x2_of(core, b)
        if n == 0:
            if isinstance(b.v, int) and b.v < 2:
                eng.wait_ge(core.E[f"x_first{b.v}"], 16)
            else:
                eng.wait_ge(core.E["x_rest"], 16)
        elif n == 1:
            core.e["x1"].wait(eng, b, apart=core.apart)
        else:
            core.e["x2"].wait(eng, b, apart=core.apart)
        for t in range(KT):
            stats.at(eng.bn_stats(core.stats[:, n, t, :], src[:, t, :]))
        for t in range(KT):
            stats.wait(eng, b, t, apart=core.apart)
            stats.at(eng.bn_aggr(core.moments[:, n, t, :], core.stats[:, n, t, :]))
    elif name == "gpsimd":
        stats.wait(eng, b, apart=core.apart)
        eps_done.at(eng.tensor_scalar(core.rstd[:, n, :], core.moments[:, n, :, 1], EPS, None, ALU.add))
        eps_done.wait(eng, b)
        rstd_done.at(eng.tensor_tensor(core.rstd[:, n, :], core.rstd[:, n, :], core.minus_half[:, :], ALU.pow))


def st_normalise(core, name, eng, b, it, n):
    rstd_done, done = core.e[f"ln{n}_rstd"], core.e[f"ln{n}"]
    if name == "vector":
        src = core.x1[:, :, :] if n == 1 else x2_of(core, b)
        dst = (core.xn, core.xn_cross, core.xn_ffn)[n]
        rstd_done.wait(eng, b)
        if n == 0:
            core.e["p_xnT"].wait(eng, b.back(1))
        elif n == 1:
            core.e["p_xcT"].wait(eng, b.back(1))
        else:
            core.e["p_xfT"].wait(eng, b.back(1))
            core.xn_stored.wait(eng, b.back(1))
        for t in range(KT):
            done.at(eng.tensor_scalar(dst[:, t, :], src[:, t, :], core.moments[:, n, t, 0:1],
                                      core.rstd[:, n, t:t + 1], ALU.subtract, ALU.mult))
    elif name == "gpsimd" and n == 0:
        bias = core.bias_row["attn", "bo"][:, :].rearrange("p (o n) -> p o n", o=1).to_broadcast([P, KT, D])
        eng.wait_ge(core.E["consts_in"], 16 * 13)
        done.wait(eng, b)
        core.e["xb"].at(eng.tensor_tensor(x2_of(core, b), x2_of(core, b), bias, ALU.add))
    elif name == "sync" and n == 0:
        core.e["p_ctxT"].wait(eng, b.back(1), apart=core.apart)
        rows = core.t["ctx_1024"].rearrange("b (t p) d -> b p t d", p=P)
        core.ctx_loaded.at(eng.dma_start(core.ctx_in[:, :, :], rows[b.v]), b)
    elif name == "sync" and n == 2:
        done.wait(eng, b, apart=core.apart)
        rows = core.xn_dram.rearrange("(b t p) d -> b p t d", p=P, t=KT)
        core.xn_stored.at(eng.dma_start(rows[b.v], core.xn_ffn[:, :, :]), b)


def st_transpose(core, name, eng, b, it, which):
    src, bank, res = {
        "xnT": (core.xn, 2, 0), "hT": (core.heads, 1, 1),
        "ctxT": (core.ctx_in, 2, 1), "xcT": (core.xn_cross, 0, 0),
    }[which]
    done, hi, lo = (core.e[x] for x in (f"p_{which}", f"{which}_hi", f"{which}_lo"))
    ps = core.psum[bank]
    if name == "tensor":
        if which == "xnT":
            if b.back(3).inside(NB):
                core.e["gate"].wait(eng, b.back(3), 0)
            else:
                core.e["ck_split"].wait(eng, b.back(1), 1)
        elif which == "hT":
            core.e["headsN"].wait(eng, b, 1)
        elif which == "ctxT":
            core.e["e1"].wait(eng, b, 1)
        elif which == "xcT":
            if b.back(2).inside(NB):
                core.e["xfT"].wait(eng, b.back(2), 0)
            elif b.back(1).inside(NB):
                core.e["m_lo"].wait(eng, b.back(1), 0)
            else:
                core.e["den"].wait(eng, b, 0)
        if which == "ctxT":
            core.ctx_loaded.wait(eng, b)
        else:
            {"xnT": core.e["ln0"], "hT": core.e["headsN"], "xcT": core.e["ln1"]}[which].wait(eng, b)
        for c in range(KT):
            for t in range(KT):
                mm = eng.transpose(ps[:, c * S + t * P:c * S + (t + 1) * P], src[:, t, c * P:(c + 1) * P],
                                   core.ident[:, :])
        done.at(mm)
    elif name == "scalar":
        done.wait(eng, b)
        if which == "xnT":
            core.e["p_cq"].wait(eng, b.back(1), 0)
        elif which == "hT":
            if b.back(-1).inside(NB):
                core.e["p_cv"].wait(eng, b.back(-1), 0)
            else:
                core.e["p_y2"].wait(eng, b.back(1), 0)
        elif which == "ctxT":
            if b.back(2).inside(NB):
                core.e["p_y2"].wait(eng, b.back(2), 0)
            else:
                core.e["p_cv"].wait(eng, b.back(1), 0)
        elif which == "xcT":
            core.e["p_y"].wait(eng, b, 0)
        hi.at(eng.activation(core.tr_hi[res][:, :, :], ps[:, :], ACT.Copy))
    elif name == "vector":
        hi.wait(eng, b)
        if which == "xnT":
            core.e["p_cq"].wait(eng, b.back(1), 0)
        elif which == "hT":
            if b.back(-1).inside(NB):
                core.e["p_cv"].wait(eng, b.back(-1), 0)
            else:
                core.e["p_y2"].wait(eng, b.back(1), 0)
        elif which == "ctxT":
            if b.back(2).inside(NB):
                core.e["p_y2"].wait(eng, b.back(2), 0)
            else:
                core.e["p_cv"].wait(eng, b.back(1), 0)
        elif which == "xcT":
            core.e["p_y"].wait(eng, b, 0)
        lo.at(eng.tensor_tensor(core.tr_lo[res][:, :, :], ps[:, :], core.tr_hi[res][:, :, :].bitcast(F32),
                                ALU.subtract))


def split_product(eng, out, left, right, skip=False, start=True, stop=True):
    terms = [(lh, rh) for (lh, _), (rh, _) in zip(left, right)]
    terms += [(lh, rl) for (lh, _), (_, rl) in zip(left, right)]
    terms += [(ll, rh) for (_, ll), (rh, _) in zip(left, right)]
    for i, (a, b) in enumerate(terms):
        mm = eng.matmul(out, a, b, start=start and i == 0, stop=stop and i == len(terms) - 1,
                        skip_group_check=skip)
    return mm


def st_project(core, name, eng, b, it, which):
    m, n, bank, tr = {
        "q": ("attn", "q", 0, 0), "k": ("attn", "k", 1, 0),
        "ck": ("xattn", "k", 2, 1), "cq": ("xattn", "q", 1, 0),
    }[which]
    hi, lo = core.hi[which], core.lo[which]
    done, rounded, split = (core.e[x] for x in (f"p_{which}", f"{which}_hi", f"{which}_split"))
    bias = core.bias_col[m, "b" + n]
    source = {"q": core.e["xnT_lo"], "k": core.e["xnT_lo"], "ck": core.e["ctxT_lo"], "cq": core.e["xcT_lo"]}[which]
    ps = core.psum[bank]
    if name == "tensor":
        if which == "q":
            core.e["xcT_lo"].wait(eng, b.back(1), 0)
        elif which == "k":
            core.e["cq_split"].wait(eng, b.back(1), 1)
        elif which == "cq":
            core.e["cv"].wait(eng, b, 1)
        elif which == "ck":
            core.e["ctxT_lo"].wait(eng, b, 0)
        source.wait(eng, b)
        w_hi, w_lo = core.w[m, "W" + n]
        for c in range(KT):
            mm = split_product(
                eng, ps[:, c * S:(c + 1) * S],
                [(w_hi[:, k, c * P:(c + 1) * P], w_lo[:, k, c * P:(c + 1) * P]) for k in range(KT)],
                [(core.tr_hi[tr][:, k, :], core.tr_lo[tr][:, k, :]) for k in range(KT)])
        done.at(mm)
    elif name == "scalar":
        done.wait(eng, b)
        if which in ("q", "k"):
            core.e["p_s1"].wait(eng, b.back(1))
        elif which == "cq":
            core.q_stacked.wait(eng, b.back(1))
        else:
            core.k_stacked.wait(eng, b.back(1))
        for c in range(KT):
            rounded.at(eng.activation(hi[:, c, :], ps[:, c * S:(c + 1) * S], ACT.Identity,
                                      bias=bias[:, c:c + 1]))
        if which in ("q", "k"):
            if which == "k":
                core.e["p_ksq"].wait(eng, b.back(1))
            dst_sq, ev = (core.q_sq, core.e["q_square"]) if which == "q" else (core.k_sq, core.e["k_square"])
            for c in range(KT):
                ev.at(eng.activation(dst_sq[:, c, :], ps[:, c * S:(c + 1) * S], ACT.Square, bias=bias[:, c:c + 1]))
    elif name == "gpsimd" and which == "q":
        core.e["q_square"].wait(eng, b)
        core.e["q_norm"].at(eng.tensor_tensor(core.q_sq[:, 0, :], core.q_sq[:, 0, :], core.q_sq[:, 1, :], ALU.add))
    elif name == "vector":
        if which == "q":
            core.e["q_square"].wait(eng, b)
        elif which == "k":
            core.e["k_square"].wait(eng, b)
        else:
            rounded.wait(eng, b)
        for c in range(KT):
            split.at(eng.scalar_tensor_tensor(lo[:, c, :], ps[:, c * S:(c + 1) * S], bias[:, c:c + 1],
                                              hi[:, c, :].bitcast(F32), ALU.add, ALU.subtract))
    elif name == "sync" and which in ("ck", "cq"):
        stack, parts, ev = ((core.q_stack, (hi, hi, lo), core.q_stacked) if which == "cq"
                            else (core.k_stack, (hi, lo, hi), core.k_stacked))
        split.wait(eng, b, apart=core.apart)
        core.e["t_tile"].wait(eng, b.back(2), apart=core.apart)
        for r, part in enumerate(parts):
            for c in range(KT):
                rows = slice(64 * b.p + r * HD, 64 * b.p + (r + 1) * HD)
                h = H // KT
                ev.at(eng.dma_start(stack[rows, c * h:(c + 1) * h, :].bitcast(F32),
                                    part[:, c, :].bitcast(F32)), b)


def st_value(core, name, eng, b, it):
    ps = core.psum[2]
    if name == "tensor":
        core.e["xnT_lo"].wait(eng, b, 0)
        w_hi, w_lo = core.w["attn", "Wv"]
        for t in range(KT):
            mm = split_product(
                eng, ps[:, t * D:(t + 1) * D],
                [(core.tr_hi[0][:, k, t * P:(t + 1) * P], core.tr_lo[0][:, k, t * P:(t + 1) * P]) for k in range(KT)],
                [(w_hi[:, k, :], w_lo[:, k, :]) for k in range(KT)])
        core.e["p_v"].at(mm)
    elif name == "vector":
        core.e["p_v"].wait(eng, b)
        core.e["v_split"].wait(eng, b.back(1))
        bias = core.bias_row["attn", "bv"][:, :].rearrange("p (o n) -> p o n", o=1).to_broadcast([P, KT, D])
        core.e["v_full"].at(eng.tensor_tensor(core.full[0][:, :, :], ps[:, :].rearrange("p (t n) -> p t n", t=KT),
                                           bias, ALU.add))
    elif name == "scalar":
        core.e["v_full"].wait(eng, b)
        core.e["p_o"].wait(eng, b.back(1))
        core.e["v_hi"].at(eng.activation(core.hi["v"][:, :, :], core.full[0][:, :, :], ACT.Copy))
    elif name == "gpsimd":
        core.e["v_hi"].wait(eng, b)
        core.e["v_split"].at(eng.tensor_tensor(core.lo["v"][:, :, :], core.full[0][:, :, :],
                                               core.hi["v"][:, :, :].bitcast(F32), ALU.subtract))


def st_key_norms(core, name, eng, b, it):
    ps = core.psum[0]
    if name == "tensor":
        if b.back(2).inside(NB):
            core.e["headsN"].wait(eng, b.back(2), 0)
        else:
            core.e["q_square"].wait(eng, b, 1)
            core.e["q_split"].wait(eng, b, 1)
        core.e["k_square"].wait(eng, b)
        for kt in range(KT):
            for c in range(KT):
                mm = eng.matmul(ps[:, kt:kt + 1], core.k_sq[:, c, kt * P:(kt + 1) * P], core.ones[:, 0:1],
                                start=c == 0, stop=c == KT - 1)
        core.e["p_ksq"].at(mm)
    elif name == "vector":
        core.e["p_ksq"].wait(eng, b)
        core.e["e1"].wait(eng, b.back(1))
        core.e["ksq"].at(eng.tensor_scalar(core.neg_ksq[:, :], ps[:, 0:KT], -1.0, None, ALU.mult))


def st_rbf(core, name, eng, b, it):
    ps = core.psum[2]
    if name == "tensor":
        core.e["v_full"].wait(eng, b, 0)
        core.e["q_split"].wait(eng, b)
        core.e["k_split"].wait(eng, b)
        core.e["q_norm"].wait(eng, b)
        for kt in range(KT):
            out = ps[:, kt * S:(kt + 1) * S]
            eng.matmul(out, core.neg_half[:, :], core.q_sq[:, 0, :], start=True, stop=False)
            rows = slice(kt * P, (kt + 1) * P)
            mm = split_product(
                eng, out, [(core.hi["k"][:, c, rows], core.lo["k"][:, c, rows]) for c in range(KT)],
                [(core.hi["q"][:, c, :], core.lo["q"][:, c, :]) for c in range(KT)], start=False)
        core.e["p_s1"].at(mm)
    elif name == "scalar":
        core.e["p_s1"].wait(eng, b)
        core.e["ksq"].wait(eng, b)
        core.e["e2"].wait(eng, b.back(1))
        for kt in range(KT):
            core.e["e1"].at(eng.activation(core.full[1][:, kt, :], ps[:, kt * S:(kt + 1) * S], ACT.Exp,
                                        bias=core.neg_ksq[:, kt:kt + 1], scale=2.0))
        core.e["e1"].wait(eng, b)
        core.e["p_den"].wait(eng, b.back(1))
        core.e["p_split"].wait(eng, b.back(1))
        core.e["e2"].at(eng.activation(core.prob[:, :, :], core.full[1][:, :, :], ACT.Exp))
        core.e["e2"].wait(eng, b)
        core.e["p_o"].wait(eng, b.back(1))
        core.e["p_hi"].at(eng.activation(core.hi["p"][:, :, :], core.prob[:, :, :], ACT.Copy))


def st_rbf_split(core, name, eng, b, it):
    if name == "vector":
        core.e["p_hi"].wait(eng, b)
        core.e["p_split"].at(eng.tensor_tensor(core.lo["p"][:, :, :], core.prob[:, :, :],
                                               core.hi["p"][:, :, :].bitcast(F32), ALU.subtract))


def st_rbf_out(core, name, eng, b, it):
    ps, den = core.psum[1], core.psum[0]
    if name == "tensor":
        if b.back(2).inside(NB):
            core.e["hT_lo"].wait(eng, b.back(2), 0)
        else:
            core.e["k_square"].wait(eng, b, 1)
            core.e["k_split"].wait(eng, b, 1)
        core.e["v_split"].wait(eng, b)
        core.e["p_split"].wait(eng, b)
        for c in range(KT):
            cols = slice(c * P, (c + 1) * P)
            mm = split_product(
                eng, ps[:, c * S:(c + 1) * S],
                [(core.hi["v"][:, kt, cols], core.lo["v"][:, kt, cols]) for kt in range(KT)],
                [(core.hi["p"][:, kt, :], core.lo["p"][:, kt, :]) for kt in range(KT)])
        core.e["p_o"].at(mm)
        if b.back(2).inside(NB):
            core.e["x2"].wait(eng, b.back(2), 0)
        else:
            core.e["ksq"].wait(eng, b, 0)
        for qt in range(KT):
            for kt in range(KT):
                mm = eng.matmul(den[:, qt:qt + 1], core.prob[:, kt, qt * P:(qt + 1) * P], core.ones[:, 0:1],
                                start=kt == 0, stop=kt == KT - 1)
        core.e["p_den"].at(mm)
    elif name == "scalar":
        core.e["p_o"].wait(eng, b)
        core.e["p_v"].wait(eng, b, 0)
        core.e["oT_hi"].at(eng.activation(core.tr_hi[0][:, :, :], ps[:, :], ACT.Copy))
    elif name == "vector":
        core.e["oT_hi"].wait(eng, b)
        core.e["oT_lo"].at(eng.tensor_tensor(core.tr_lo[0][:, :, :], ps[:, :], core.tr_hi[0][:, :, :].bitcast(F32),
                                          ALU.subtract))
        core.e["p_den"].wait(eng, b)
        core.e["den"].at(eng.reciprocal(core.r_den[:, :], den[:, 0:KT]))


def st_self_output(core, name, eng, b, it):
    ps = core.psum[1]
    if name == "tensor":
        core.e["oT_lo"].wait(eng, b, 0)
        core.e["oT_lo"].wait(eng, b)
        w_hi, w_lo = core.w["attn", "Wo"]
        for t in range(KT):
            rows = slice(t * P, (t + 1) * P)
            mm = split_product(
                eng, ps[:, t * D:(t + 1) * D],
                [(core.tr_hi[0][:, c, rows], core.tr_lo[0][:, c, rows]) for c in range(KT)],
                [(w_hi[:, c, :], w_lo[:, c, :]) for c in range(KT)])
        core.e["p_y"].at(mm)
    elif name == "vector":
        core.e["p_y"].wait(eng, b)
        core.e["den"].wait(eng, b)
        core.e["xb"].wait(eng, b)
        core.e["resid1"].wait(eng, b.back(1))
        for t in range(KT):
            core.e["x1"].at(eng.scalar_tensor_tensor(core.x1[:, t, :], ps[:, t * D:(t + 1) * D],
                                                  core.r_den[:, t:t + 1], x2_of(core, b)[:, t, :],
                                                  ALU.mult, ALU.add))
    elif name == "gpsimd":
        core.e["x1"].wait(eng, b, apart=core.apart)
        bias = core.bias_row["xattn", "bo"][:, :].rearrange("p (o n) -> p o n", o=1).to_broadcast([P, KT, D])
        core.e["resid1"].at(eng.tensor_tensor(x2_of(core, b), core.x1[:, :, :], bias, ALU.add))


def st_cross_value(core, name, eng, b, it):
    ps = core.psum[1]
    if name == "tensor":
        core.e["x1"].wait(eng, b, 1)
        w_hi, w_lo = core.w["xattn", "Wv"]
        for t in range(KT):
            rows = slice(t * P, (t + 1) * P)
            mm = split_product(
                eng, ps[:, t * D:(t + 1) * D],
                [(core.tr_hi[1][:, c, rows], core.tr_lo[1][:, c, rows]) for c in range(KT)],
                [(w_hi[:, c, :], w_lo[:, c, :]) for c in range(KT)])
        core.e["p_cv"].at(mm)
    elif name == "vector":
        core.e["p_cv"].wait(eng, b)
        core.e["av"].wait(eng, b.back(2))
        for t in range(KT):
            core.e["cv"].at(eng.tensor_tensor(
                core.v_aug[b.p][:, t, :, 0:HD], ps[:, t * D:(t + 1) * D].rearrange("p (h d) -> p h d", h=H),
                core.bias_row["xattn", "bv"][:, :].rearrange("p (h d) -> p h d", h=H), ALU.add))


def st_scores(core, name, eng, b, it, i):
    base = 64 * b.p
    for qt in range(KT):
        n = 2 * i + qt
        ps = core.psum[3 + n % 4]
        if name == "tensor":
            if n == 0:
                core.q_stacked.wait(eng, b)
                core.k_stacked.wait(eng, b)
            if n >= 4:
                core.e["maxed"].wait(eng, b, n - 4)
            else:
                core.e["exp"].wait(eng, b.back(1), 12 + n)
            eng.matmul(ps[:, :], core.ident_bf[:, :],
                       core.mask_q[:, qt:qt + 1, :].to_broadcast([P, 2, S]), start=True, stop=False,
                       skip_group_check=True)
            for h in range(2):
                mm = eng.matmul(ps[:, h * S:(h + 1) * S],
                                core.q_stack[base:base + 3 * HD, 2 * i + h, qt * P:(qt + 1) * P],
                                core.k_stack[base:base + 3 * HD, 2 * i + h, :], start=False, stop=True,
                                skip_group_check=True)
            core.e["s_tile"].at(mm)
        elif name == "vector":
            core.e["s_tile"].wait(eng, b, n)
            if n == 0:
                core.e["p_max"].wait(eng, b.back(1))
            core.e["maxed"].at(eng.tensor_reduce(core.neg_max[:, qt, 2 * i:2 * i + 2],
                                              ps[:, :].rearrange("p (h k) -> p h k", h=2), AX.X, ALU.max,
                                              negate=True))


def st_maxima(core, name, eng, b, it):
    ps = core.psum[0]
    if name == "tensor":
        if b.back(-1).inside(NB):
            core.e["den"].wait(eng, b.back(-1), 0)
        else:
            core.e["x2"].wait(eng, b.back(1), 0)
        core.e["maxed"].wait(eng, b)
        for qt in range(KT):
            mm = eng.transpose(ps[0:H, qt * P:(qt + 1) * P], core.neg_max[:, qt, :], core.ident[:, :])
        core.e["p_max"].at(mm)
    elif name == "scalar":
        core.e["p_max"].wait(eng, b)
        core.m["stacked"].wait(eng, b.back(1))
        core.e["m_hi"].at(eng.activation(core.max_hi[0:H, :], ps[0:H, 0:S], ACT.Copy))
    elif name == "vector":
        core.e["m_hi"].wait(eng, b)
        core.e["m_lo"].at(eng.tensor_tensor(core.max_lo[0:H, :], ps[0:H, 0:S], core.max_hi[0:H, :].bitcast(F32),
                                         ALU.subtract))
    elif name == "sync":
        for r, part in enumerate((core.max_hi, core.max_lo)):
            if r == 0:
                core.e["m_hi"].wait(eng, b)
                core.e["s_tile"].wait(eng, b)
            else:
                core.e["m_lo"].wait(eng, b)
            row = 64 * b.p + 3 * HD + r
            core.m["stacked"].at(eng.dma_start(core.q_stack[row:row + 1, :, :].bitcast(F32),
                                            part[0:H, :].bitcast(F32)), b)


def st_exps(core, name, eng, b, it, i):
    base = 64 * b.p
    for kt in range(KT):
        n = 2 * i + kt
        ps = core.psum[3 + n % 4]
        if name == "tensor":
            if n == 0:
                core.m["stacked"].wait(eng, b)
            if n >= 4:
                core.e["exp"].wait(eng, b, n - 4)
            else:
                core.e["maxed"].wait(eng, b, 12 + n)
            for h in range(2):
                eng.matmul(ps[:, h * S:(h + 1) * S],
                           core.k_stack[base:base + 3 * HD + 2, 2 * i + h, kt * P:(kt + 1) * P],
                           core.q_stack[base:base + 3 * HD + 2, 2 * i + h, :], start=h == 0, stop=False,
                           skip_group_check=True)
            mm = eng.matmul(ps[:, :], core.ident_bf[:, :],
                            core.mask_k[:, kt:kt + 1, :].to_broadcast([P, 2, S]), start=False, stop=True,
                            skip_group_check=True)
            core.e["t_tile"].at(mm)
        elif name == "scalar":
            core.e["t_tile"].wait(eng, b, n)
            if n % 4 == 0:
                g = n // 4
                if g >= 2:
                    core.e["av"].wait(eng, b, g - 2)
                else:
                    core.e["av"].wait(eng, b.back(1), g + 2)
            core.e["exp"].at(eng.activation(core.exp_ring[:, n % 8, :, :], ps[:, :], ACT.Exp, scale=HD ** -0.5))


def st_weighted(core, name, eng, b, it, g):
    ps = core.psum[7]
    if name == "tensor":
        if g == 0:
            core.e["cv"].wait(eng, b)
        if g == 2:
            core.e["av_out"].wait(eng, b, 0)
        if g == 0:
            core.e["av_out"].wait(eng, b.back(1), 1)
        core.e["exp"].wait(eng, b, 4 * g + 3)
        for kt in range(KT):
            for q in range(4):
                tile = 2 * (2 * g + q // 2) + kt
                mm = eng.matmul(ps[32 * q:32 * q + 32, (g % 2) * S:(g % 2 + 1) * S],
                                core.v_aug[b.p][:, kt, 4 * g + q, :], core.exp_ring[:, tile % 8, q % 2, :],
                                start=kt == 0, stop=kt == KT - 1, skip_group_check=True)
        core.e["av"].at(mm)
    elif name == "scalar" and g % 2 == 1:
        core.e["av"].wait(eng, b, g)
        if g == 1:
            core.e["p_headsT"].wait(eng, b.back(1))
        core.e["av_out"].at(eng.activation(core.heads_t[:, g - 1:g + 1, :], ps[:, :], ACT.Copy))


def st_heads_transposed(core, name, eng, b, it):
    for qt in range(KT):
        ps = core.psum[qt]
        if name == "tensor":
            if qt == 0:
                if b.back(-2).inside(NB):
                    core.e["q_square"].wait(eng, b.back(-2), 1)
                    core.e["q_split"].wait(eng, b.back(-2), 1)
                elif b.back(-1).inside(NB):
                    core.e["xcT_lo"].wait(eng, b.back(-1), 0)
                else:
                    core.e["xfT"].wait(eng, b.back(1), 0)
            elif qt == 1:
                if b.back(-2).inside(NB):
                    core.e["k_square"].wait(eng, b.back(-2), 1)
                    core.e["k_split"].wait(eng, b.back(-2), 1)
                elif b.back(-1).inside(NB):
                    core.e["cq_split"].wait(eng, b.back(-1), 1)
                else:
                    core.e["hT_lo"].wait(eng, b.back(1), 0)
            core.e["av_out"].wait(eng, b)
            for g in range(4):
                mm = eng.transpose(ps[:, g * P:(g + 1) * P], core.heads_t[:, g, qt * P:(qt + 1) * P],
                                   core.ident[:, :])
            core.e["p_headsT"].at(mm)
        elif name == "vector":
            core.e["p_headsT"].wait(eng, b, qt)
            view = ps[:, :].rearrange("p (h d) -> p h d", h=H)
            core.e["r_heads"].at(eng.reciprocal(core.r_heads[:, qt, :], view[:, :, HD]))
            core.e["r_heads"].wait(eng, b, qt)
            if qt == 0:
                core.e["p_hT"].wait(eng, b.back(1))
            scale = core.r_heads[:, qt, :].rearrange("p (h o) -> p h o", o=1).to_broadcast([P, H, HD])
            core.e["headsN"].at(eng.tensor_tensor(core.heads[:, qt, :].rearrange("p (h d) -> p h d", h=H),
                                               view[:, :, 0:HD], scale, ALU.mult))


def st_output(core, name, eng, b, it):
    ps = core.psum[0]
    if name == "tensor":
        if b.back(-2).inside(NB):
            core.e["ksq"].wait(eng, b.back(-2), 0)
        else:
            core.e["headsN"].wait(eng, b, 0)
        core.e["hT_lo"].wait(eng, b)
        w_hi, w_lo = core.w["xattn", "Wo"]
        for t in range(KT):
            rows = slice(t * P, (t + 1) * P)
            mm = split_product(
                eng, ps[:, t * D:(t + 1) * D],
                [(core.tr_hi[1][:, c, rows], core.tr_lo[1][:, c, rows]) for c in range(KT)],
                [(w_hi[:, c, :], w_lo[:, c, :]) for c in range(KT)])
        core.e["p_y2"].at(mm)
    elif name == "vector":
        core.e["p_y2"].wait(eng, b)
        core.e["resid1"].wait(eng, b)
        core.e["x2"].at(eng.tensor_tensor(x2_of(core, b), ps[:, :].rearrange("p (t n) -> p t n", t=KT),
                                       x2_of(core, b), ALU.add))


def st_router_transpose(core, name, eng, b, it):
    ps = core.psum[0]
    if name == "tensor":
        if b.back(-1).inside(NB):
            core.e["m_lo"].wait(eng, b.back(-1), 0)
        else:
            core.e["x2"].wait(eng, b, 0)
        core.e["ln2"].wait(eng, b)
        for c in range(KT):
            for t in range(KT):
                mm = eng.transpose(ps[:, c * S + t * P:c * S + (t + 1) * P],
                                   core.xn_ffn[:, t, c * P:(c + 1) * P], core.ident[:, :])
        core.e["p_xfT"].at(mm)
    elif name == "scalar":
        core.e["p_xfT"].wait(eng, b)
        core.e["p_gate"].wait(eng, b.back(1))
        core.e["xfT"].at(eng.activation(core.q_sq[:, :, :], ps[:, :], ACT.Copy))


def st_router(core, name, eng, b, it):
    ps = core.psum[2]
    if name == "tensor":
        if b.back(-2).inside(NB):
            core.e["ck_split"].wait(eng, b.back(-2), 1)
        else:
            core.e["gate"].wait(eng, b.back(1), 0)
        core.e["xfT"].wait(eng, b)
        for t in range(KT):
            for c in range(KT):
                mm = eng.matmul(ps[:, t * NE:(t + 1) * NE], core.q_sq[:, c, t * P:(t + 1) * P],
                                core.gate_w[:, c, :], start=c == 0, stop=c == KT - 1)
        core.e["p_gate"].at(mm)
    elif name == "vector":
        core.e["p_gate"].wait(eng, b)
        core.e["gate"].at(eng.tensor_copy(core.logits[:, bass.ds(b.v * KT, KT), :],
                                       ps[:, 0:KT * NE].rearrange("p (t n) -> p t n", t=KT)))


def attention_over(core, eng):
    last = Step(3, 1)
    core.e["gate"].wait(eng, last)
    core.e["xfT"].wait(eng, last)
    core.e["ln2_rstd"].wait(eng, last)
    core.e["resid1"].wait(eng, last)
    for b in (last.back(1), last):
        core.xn_stored.wait(eng, b)


def routing_sync(core, e):
    t, r = core.t, core.r
    for x in range(NE):
        rows = t["L0_ffn_b1"][NE - 1 - x].rearrange("(f p) -> f p", p=P)
        e.dma_start(core.b1_rows[x * FT:(x + 1) * FT, :], rows).then_inc(r["b1_in"], 16)
    for x in range(NE):
        row = t["L0_ffn_b2"][NE - 1 - x:NE - x, :]
        loads(core, e, core.b2_row[:, x * D:(x + 1) * D], row.partition_broadcast(P), core.E["experts_b"])
    for x in range(EARLY, NE):
        e.wait_ge(core.E["experts_in"], 32 * x)
        load_expert(core, e, x, core.E["experts_in"])


def load_expert(core, eng, x, sem):
    place = core.experts_w[:, (NE - 1 - x) * PLACE:(NE - x) * PLACE]
    for n, part in (("W1", place[:, 0:KT * FF]), ("W2", place[:, KT * FF:])):
        k = KT if n == "W1" else FT
        loads(core, eng, part.rearrange("p (k n) -> p k n", k=k),
                   core.t[f"L0_ffn_{n}"][x].rearrange("(k p) n -> p k n", p=P), sem)


def routing_gpsimd(core, e):
    pool = core.r["pool"]
    e.iota(core.iota_i[:, :], pattern=[[1, P]], base=0, channel_multiplier=0).then_inc(pool, 1)
    e.iota(core.iota_p[:, :], pattern=[[P, TT]], base=1, channel_multiplier=1).then_inc(pool, 1)
    e.wait_ge(pool, 2)
    e.tensor_copy(core.iota_f[:, :], core.iota_i[:, :]).then_inc(pool, 1)
    e.tensor_copy(core.token_f[:, 0, :], core.iota_p[:, :]).then_inc(pool, 1)
    e.wait_ge(pool, 4)
    e.tensor_scalar(core.token_f[:, 1, :], core.token_f[:, 0, :], float(NB * S), None, ALU.add).then_inc(pool, 1)
    e.affine_select(out=core.strict[:, :], in_=core.ones[:, :], compare_op=ALU.is_gt, fill=0.0, base=0,
                    pattern=[[1, P]], channel_multiplier=-1).then_inc(pool, 1)


def routing_scalar(core, e):
    e.wait_ge(core.r["delta"], 1)
    e.activation(core.ex[:, :], core.delta[:, :], ACT.Exp).then_inc(core.r["ex"], 1)


def routing_tensor(core, e):
    r = core.r
    e.wait_ge(r["pool"], 6)
    e.wait_ge(r["both"], 1)
    flat = core.both[:, :, :].rearrange("p t e -> p (t e)")
    e.matmul(core.psum[0][:, 0:TT * NE], core.strict[:, :], flat, start=True, stop=True)
    e.matmul(core.psum[1][:, 0:TT * NE], core.ones[:, :], flat, start=True, stop=True).then_inc(r["prefix"], 1)
    e.wait_ge(r["b1_in"], 16 * NE)
    n = NE * FT
    e.transpose(core.psum[3][:, 0:n], core.b1_rows[0:n, :], core.ident[0:n, 0:n]).then_inc(r["b1_t"], 1)
    for c in range(4):
        e.wait_ge(r["slots"], c + 1)
        for tt in range(TT // 2):
            mm = e.matmul(core.psum[2][:, 0:3 * COLS], core.row_hot[c % 2][:, tt, :],
                          core.tile_vals[c % 2][:, tt, :, :].rearrange("p a t -> p (a t)"),
                          start=c == 0 and tt == 0, stop=c == 3 and tt == TT // 2 - 1)
        mm.then_inc(r["table"], 1)
    e.wait_ge(r["idx"], 1)


def best_experts(core, e, first, last):
    best = core.r["best"]
    for tt in range(first, last):
        e.max(core.top8[:, tt, :], core.logits[:, tt, :]).then_inc(best, 1)
    for tt in range(first, last):
        e.wait_ge(best, first + tt + 1)
        e.max_index(core.idx8[:, tt, :], core.top8[:, tt, :], core.logits[:, tt, :]).then_inc(best, 1)


def routing_vector(core, e):
    r = core.r
    count = [0]

    def link(inst):
        inst.then_inc(r["vec"], 1)
        count[0] += 1
        return inst

    def settle():
        e.wait_ge(r["vec"], count[0])

    def bc(ap, shape, dim):
        return ap.unsqueeze(dim).to_broadcast(shape)

    best_experts(core, e, TT - KT, TT)
    e.wait_ge(r["best"], 2 * TT)
    e.tensor_tensor(core.delta[:, :], core.top8[:, :, 1], core.top8[:, :, 0], ALU.subtract)\
        .then_inc(r["delta"], 1)
    settle()
    link(e.tensor_copy(core.choice[:, :, :], core.idx8[:, :, 0:2]))
    settle()
    e.wait_ge(r["pool"], 6)
    for j in range(2):
        link(e.tensor_tensor(core.onehot[:, j, :, :], bc(core.iota_f[:, 0:NE], [P, TT, NE], 1),
                             bc(core.choice[:, :, j], [P, TT, NE], 2), ALU.is_equal))
    settle()
    e.tensor_tensor(core.both[:, :, :], core.onehot[:, 0, :, :], core.onehot[:, 1, :, :], ALU.add)\
        .then_inc(r["both"], 1)
    e.wait_ge(r["ex"], 1)
    link(e.tensor_scalar(core.one_plus[:, :], core.ex[:, :], 1.0, None, ALU.add))
    settle()
    link(e.reciprocal(core.weight[:, 0, :], core.one_plus[:, :]))
    settle()
    link(e.tensor_tensor(core.weight[:, 1, :], core.ex[:, :], core.weight[:, 0, :], ALU.mult))
    e.wait_ge(r["prefix"], 1)
    totals = core.psum[1][:, 0:TT * NE].rearrange("p (t e) -> p t e", e=NE)
    within = core.psum[0][:, 0:TT * NE].rearrange("p (t e) -> p t e", e=NE)
    link(e.tensor_copy(core.running[0][:, :, :], totals))
    settle()
    src, dst = core.running
    shift = 1
    while shift < TT:
        link(e.tensor_copy(dst[:, 0:shift, :], src[:, 0:shift, :]))
        link(e.tensor_tensor(dst[:, shift:, :], src[:, shift:, :], src[:, 0:TT - shift, :], ALU.add))
        settle()
        src, dst = dst, src
        shift *= 2
    link(e.scalar_tensor_tensor(out=core.cmp16[:, :, :], in0=bc(src[:, TT - 1, :], [P, NE, 16], 2),
                                scalar=1.0 / P, in1=bc(core.iota_f[:, 0:16], [P, NE, 16], 1),
                                op0=ALU.mult, op1=ALU.is_gt))
    link(e.tensor_tensor(core.slot_of[:, :, :], src[:, :, :], totals, ALU.subtract))
    settle()
    link(e.tensor_reduce(core.own_tiles[:, :], core.cmp16[:, :, :], AX.X, ALU.add))
    link(e.tensor_tensor(core.slot_of[:, :, :], core.slot_of[:, :, :], within, ALU.add))
    settle()
    src, dst = core.tiles_of
    link(e.tensor_copy(src[:, :], core.own_tiles[:, :]))
    settle()
    shift = 1
    while shift < NE:
        link(e.tensor_copy(dst[:, 0:shift], src[:, 0:shift]))
        link(e.tensor_tensor(dst[:, shift:], src[:, shift:], src[:, 0:NE - shift], ALU.add))
        settle()
        src, dst = dst, src
        shift *= 2
    n = MAX_TILES + 1
    link(e.tensor_tensor(core.cmp_tiles[:, :, :], bc(core.iota_f[:, 0:n], [P, n, NE - 1], 2),
                         bc(src[:, 0:NE - 1], [P, n, NE - 1], 1), ALU.is_ge))
    link(e.tensor_tensor(core.first_slot[:, :], src[:, :], core.own_tiles[:, :], ALU.subtract))
    settle()
    link(e.tensor_reduce(core.expert_f[:, :], core.cmp_tiles[:, :, :], AX.X, ALU.add))
    settle()
    link(e.tensor_scalar(core.expert_f[:, :], core.expert_f[:, :], -1.0, float(NE - 1), ALU.mult, ALU.add))
    settle()
    link(e.tensor_copy(core.tile_expert[:, :], core.expert_f[:, :]))
    link(e.tensor_scalar(core.loads_f[:, :], core.expert_f[:, :], float(NE - EARLY), -32.0, ALU.min, ALU.mult))
    settle()
    link(e.tensor_scalar(core.loads_f[:, :], core.loads_f[:, :], 32.0 * NE, None, ALU.add))
    settle()
    link(e.tensor_copy(core.tile_loads[:, :], core.loads_f[:, :]))
    link(e.scalar_tensor_tensor(out=core.slot_of[:, :, :], in0=bc(core.first_slot[:, :], [P, TT, NE], 1),
                                scalar=float(P), in1=core.slot_of[:, :, :], op0=ALU.mult, op1=ALU.add))
    settle()
    for j in range(2):
        link(e.tensor_tensor(core.picked[:, :, :], core.slot_of[:, :, :], core.onehot[:, j, :, :], ALU.mult))
        settle()
        link(e.tensor_reduce(core.slot[:, j, :], core.picked[:, :, :], AX.X, ALU.add))
        settle()
    link(e.tensor_copy(core.slot_int[:, :, :], core.slot[:, :, :]))
    settle()
    link(e.tensor_scalar(core.tile_int[:, :, :], core.slot_int[:, :, :], 7, None, ALU.logical_shift_right))
    link(e.tensor_scalar(core.row_int[:, :, :], core.slot_int[:, :, :], P - 1, None, ALU.bitwise_and))
    settle()
    link(e.tensor_copy(core.slot_tile[:, :, :], core.tile_int[:, :, :]))
    link(e.tensor_copy(core.slot_row[:, :, :], core.row_int[:, :, :]))
    link(e.tensor_copy(core.weight_hi[:, :, :], core.weight[:, :, :]))
    settle()
    link(e.tensor_tensor(core.weight_lo[:, :, :], core.weight[:, :, :], core.weight_hi[:, :, :].bitcast(F32),
                         ALU.subtract))
    settle()
    for c in range(4):
        j, tiles, buf = c // 2, slice(c % 2 * TT // 2, (c % 2 + 1) * TT // 2), c % 2
        if c >= 1:
            e.wait_ge(r["slots"], c)
        if c >= 2:
            e.wait_ge(r["table"], c - 1)
        e.tensor_tensor(core.row_hot[buf][:, :, :], bc(core.iota_f[:, :], [P, TT // 2, P], 1),
                        bc(core.slot_row[:, j, tiles], [P, TT // 2, P], 2), ALU.is_equal)
        link(e.tensor_tensor(core.tile_hot[:, :, :], bc(core.iota_f[:, 0:COLS], [P, TT // 2, COLS], 1),
                             bc(core.slot_tile[:, j, tiles], [P, TT // 2, COLS], 2), ALU.is_equal))
        settle()
        for a, val in enumerate((core.token_f[:, j, tiles], core.weight_hi[:, j, tiles].bitcast(F32),
                                 core.weight_lo[:, j, tiles])):
            last = e.tensor_tensor(core.tile_vals[buf][:, :, a, :], core.tile_hot[:, :, :],
                                   bc(val, [P, TT // 2, COLS], 2), ALU.mult)
            if a < 2:
                link(last)
        last.then_inc(r["slots"], 1)
        settle()
    e.wait_ge(r["b1_t"], 1)
    e.tensor_copy(core.b1_cols[:, :], core.psum[3][:, 0:NE * FT]).then_inc(r["b1_cols"], 1)
    e.wait_ge(r["table"], 4)
    link(e.tensor_copy(core.slot_id[:, :], core.psum[2][:, 0:MAX_TILES]))
    link(e.tensor_copy(core.slot_weight[:, :], core.psum[2][:, COLS:COLS + MAX_TILES]))
    settle()
    link(e.tensor_tensor(core.slot_weight[:, :], core.slot_weight[:, :],
                         core.psum[2][:, 2 * COLS:2 * COLS + MAX_TILES], ALU.add))
    tmp = core.slot_tmp
    link(e.tensor_scalar(tmp[:, 0, :], core.slot_id[:, :], -1.0, 0.0, ALU.add, ALU.max))
    link(e.tensor_scalar(tmp[:, 1, :], core.slot_id[:, :], float(NB * S), float(NB * S), ALU.is_gt, ALU.mult))
    link(e.tensor_scalar(tmp[:, 2, :], core.slot_id[:, :], 0.0, 4.0 * NB * S, ALU.is_equal, ALU.mult))
    settle()
    link(e.tensor_tensor(core.gather_idx[:, :], tmp[:, 0, :], tmp[:, 1, :], ALU.subtract))
    link(e.scalar_tensor_tensor(out=core.scatter_idx[:, :], in0=core.slot_id[:, :], scalar=-1.0,
                                in1=tmp[:, 2, :], op0=ALU.add, op1=ALU.add))
    settle()
    e.tensor_copy(core.slot_tmp[:, 3, :], core.slot_id[:, :]).then_inc(r["idx"], 1)
    e.wait_ge(core.E["experts_b"], 16 * NE)


def experts(core, name, eng, it):
    def at(lag, fn):
        b = it.back(lag)
        if b.inside(MAX_TILES):
            fn(core, name, eng, b)

    if name == "gpsimd":
        if isinstance(it.v, int) and it.v == 0:
            eng.wait_ge(core.r["idx"], 1)
        at(0, ex_gather)
        at(4, ex_scatter)
        return
    at(1, ex_weights)
    at(1, ex_rows_t)
    at(2, ex_hidden)
    at(3, ex_out)


def expert_of(core, eng, b):
    return eng.value_load(core.tile_expert[0:1, bass.ds(b.v, 1)], min_val=0, max_val=NE - 1)


def ex_gather(core, name, eng, b):
    core.rows_in.wait(eng, b.back(2), apart=core.apart)
    core.m["gnow"].at(eng.tensor_copy(core.gather_now[b.p][:, :], core.gather_idx[:, bass.ds(b.v, 1)]))
    core.m["gnow"].wait(eng, b, apart=core.apart)
    core.m["xT"].wait(eng, b.back(2), apart=core.apart)
    core.rows_in.at(eng.indirect_dma_start(
        core.slots_in[b.p][:, :], None, core.xn_dram,
        bass.IndirectOffsetOnAxis(ap=core.gather_now[b.p][:, :], axis=0)), b)


def ex_scatter(core, name, eng, b):
    core.rows_out.wait(eng, b.back(2), apart=core.apart)
    core.m["snow"].at(eng.tensor_copy(core.scatter_now[b.p][:, :], core.scatter_idx[:, bass.ds(b.v, 1)]))
    core.m["snow"].wait(eng, b, apart=core.apart)
    core.m["y"].wait(eng, b, apart=core.apart)
    core.rows_out.at(eng.indirect_dma_start(
        core.choice_dram, bass.IndirectOffsetOnAxis(ap=core.scatter_now[b.p][:, :], axis=0),
        core.y[b.p][:, :], None, bounds_check=2 * NB * S - 1, oob_is_err=False), b)


def ex_rows_t(core, name, eng, b):
    ps = core.psum[0]
    if name == "tensor":
        core.rows_in.wait(eng, b)
        core.m["slots_t"].wait(eng, b.back(1))
        for c in range(KT):
            mm = eng.transpose(ps[:, c * P:(c + 1) * P], core.slots_in[b.p][:, c * P:(c + 1) * P],
                               core.ident[:, :])
        core.m["xT"].at(mm)
    elif name == "scalar":
        core.m["xT"].wait(eng, b)
        core.m["hid"].wait(eng, b.back(2))
        core.m["slots_t"].at(eng.activation(core.slots_t[b.p][:, :, :], ps[:, 0:KT * P], ACT.Copy))

def ex_weights(core, name, eng, b):
    if name == "vector":
        x = expert_of(core, eng, b)
        loads_due = eng.value_load(core.tile_loads[0:1, bass.ds(b.v, 1)], min_val=32 * EARLY, max_val=32 * NE)
        eng.wait_ge(core.E["experts_in"], loads_due)
        core.m["hid"].wait(eng, b.back(2))
        core.m["w1"].at(eng.tensor_copy(core.w1_now[b.p][:, :], core.experts_w[:, bass.ds(x * PLACE, KT * FF)]))


def ex_hidden(core, name, eng, b):
    half_tiles = FT // 2
    banks = [core.psum[1 + 2 * b.p + half] for half in range(2)]
    if name == "tensor":
        core.m["w1"].wait(eng, b)
        core.m["slots_t"].wait(eng, b)
        for half in range(2):
            (core.m["act_a"], core.m["act_v"])[half].wait(eng, b.back(2))
            for f in range(half_tiles):
                for c in range(KT):
                    start = c * FF + (half * half_tiles + f) * P
                    mm = eng.matmul(banks[half][:, f * P:(f + 1) * P], core.w1_now[b.p][:, start:start + P],
                                    core.slots_t[b.p][:, c, :], start=c == 0, stop=c == KT - 1)
            core.m["hid"].at(mm)
    elif name == "vector":
        x = expert_of(core, eng, b)
        core.m["act_a"].wait(eng, b.back(2))
        core.m["b1t"].at(eng.tensor_copy(core.b1_tile[b.p][:, :], core.b1_cols[:, bass.ds(x * FT, FT)]))
        core.m["b1t"].wait(eng, b)
        core.m["hid"].wait(eng, b, 1)
        core.m["out"].wait(eng, b.back(2))
        for f in range(half_tiles):
            g = half_tiles + f
            core.m["act_v"].at(eng.tensor_scalar(core.hid_t[b.p][:, g, :], banks[1][:, f * P:(f + 1) * P],
                                                 core.b1_tile[b.p][:, g:g + 1], 0.0, ALU.add, ALU.max))
    elif name == "scalar":
        core.m["b1t"].wait(eng, b)
        core.m["hid"].wait(eng, b, 0)
        core.m["out"].wait(eng, b.back(2))
        for f in range(half_tiles):
            core.m["act_a"].at(eng.activation(core.hid_t[b.p][:, f, :], banks[0][:, f * P:(f + 1) * P],
                                              ACT.Relu, bias=core.b1_tile[b.p][:, f:f + 1]))


def ex_out(core, name, eng, b):
    ps = core.psum[5 + b.p]
    if name == "tensor":
        x = expert_of(core, eng, b)
        core.m["act_a"].wait(eng, b)
        core.m["act_v"].wait(eng, b)
        core.m["y"].wait(eng, b.back(2), 0)
        for f in range(FT):
            mm = eng.matmul(ps[:, 0:D], core.hid_t[b.p][:, f, :],
                            core.experts_w[:, bass.ds(x * PLACE + (KT * FF + f * D), D)],
                            start=f == 0, stop=f == FT - 1)
        core.m["out"].at(mm)
    elif name == "vector":
        x = expert_of(core, eng, b)
        core.m["out"].wait(eng, b)
        core.rows_out.wait(eng, b.back(2))
        core.m["y"].at(eng.tensor_tensor(core.y[b.p][:, :], ps[:, 0:D], core.b2_row[:, bass.ds(x * D, D)], ALU.add))
        core.m["y"].wait(eng, b, 0)
        core.m["y"].at(eng.tensor_scalar(core.y[b.p][:, :], core.y[b.p][:, :],
                                      core.slot_weight[:, bass.ds(b.v, 1)], None, ALU.mult))


def finish_gpsimd(core, e):
    pass


def finish_scalar(core, e):
    pass


def finish_tensor(core, e):
    pass


def finish_sync(core, e):
    for i in (MAX_TILES - 2, MAX_TILES - 1):
        core.rows_out.wait(e, Step(i // 2, i % 2))
    core.m["out"].wait(e, Step((MAX_TILES - 1) // 2, (MAX_TILES - 1) % 2))
    rows = core.choice_dram.rearrange("(j t p) d -> p j t d", j=2, p=P)
    out = core.out.rearrange("b (t p) d -> p (b t) d", p=P)
    for c in range(CHUNKS):
        tiles = slice(c * CHUNK, (c + 1) * CHUNK)
        for j in range(2):
            e.dma_start(core.choice_rows[c][:, j, :, :], rows[:, j, tiles, :]).then_inc(core.choice_in[c], 16)
    for c in range(CHUNKS):
        tiles = slice(c * CHUNK, (c + 1) * CHUNK)
        e.wait_ge(core.sums, 2 * (c + 1))
        e.dma_start(out[:, tiles, :], core.x2[:, tiles, :]).then_inc(core.stored, 16)
    e.wait_ge(core.stored, 16 * CHUNKS)


def finish_vector(core, e):
    for c in range(CHUNKS):
        rows = core.x2[:, c * CHUNK:(c + 1) * CHUNK, :]
        for j in range(2):
            if j == 0:
                e.wait_ge(core.choice_in[c], 32)
            else:
                e.wait_ge(core.sums, 2 * c + 1)
            e.tensor_tensor(rows, rows, core.choice_rows[c][:, j, :, :], ALU.add).then_inc(core.sums, 1)


INPUTS = ["x", "ctx_1024", "mask_1x1xSxS2_ik0"] + [
    f"L0_{m}_{n}" for m in ("attn", "xattn") for n in ("Wq", "bq", "Wk", "bk", "Wv", "bv", "Wo", "bo")] + [
    f"L0_ffn_{n}" for n in ("Wg", "W1", "b1", "W2", "b2")]


def kernel(**inputs):
    import numpy as np
    import concourse.bacc as bacc
    from concourse.bass_utils import run_bass_kernel_spmd

    nc = bacc.Bacc("TRN2", target_bir_lowering=False, num_devices=1)
    arrays = {n: np.ascontiguousarray(inputs[n]) for n in INPUTS}
    handles = {n: nc.dram_tensor(n, a.shape, mybir.dt.from_np(a.dtype), kind="ExternalInput").ap()
               for n, a in arrays.items()}
    out = nc.dram_tensor("out", (NB, S, D), F32, kind="ExternalOutput").ap()
    build(nc, handles, out)
    result = run_bass_kernel_spmd(nc, [arrays], core_ids=[0])
    return result.results[0]["out"]
```
